# Optimizing a Trainium2 kernel written in Bass

```python
import numpy as np
import jax
import jax.numpy as jnp

def _softmax(x, axis=-1):
    return jax.nn.softmax(x, axis=axis)

def _gelu(x):
    return jax.nn.gelu(x, approximate=True)

def _silu(x):
    return jax.nn.silu(x)

def _sigmoid(x):
    return jax.nn.sigmoid(x)

def _layernorm(x, axis=-1, eps=1e-05):
    m = jnp.mean(x, axis=axis, keepdims=True)
    v = jnp.var(x, axis=axis, keepdims=True)
    return (x - m) / jnp.sqrt(v + eps)

def _scatter_add(tgt, idx, src, axis=0):
    return tgt.at[idx].add(src)

def _segment_sum(src, seg, n):
    return jax.ops.segment_sum(src, seg, n)
kernel_name = 'mk_dlrm_tower_d1_rec_r8_f18276'

def setup_inputs(seed: int=0):
    np.random.seed(seed)
    _w = jnp.asarray

    def _rec_inputs():
        import jax
        import jax.numpy as jnp
        _tk = jax.random.key(seed)
        dense_ctx = jax.random.normal(jax.random.fold_in(_tk, 190), (512, 16), jnp.float32)
        ids = jnp.stack([jax.random.randint(jax.random.fold_in(_tk, 200 + f), (512,), 0, v, jnp.int32) for f, v in enumerate([1000, 1250, 125000, 1000, 12500, 125000, 1250, 125000, 125000, 125000, 12500, 1000, 125000, 125000, 125000, 1000, 12500, 125000, 1250, 1250, 1250, 125000, 1000, 125000, 125000, 1250, 125000, 1250, 1250, 12500, 12500, 12500, 12500, 125000, 12500, 12500, 1000, 1250, 1000, 12500, 1000, 1250, 1250, 1000, 1250, 1250, 12500, 12500, 1250, 1000, 1000, 12500, 12500, 1000, 1000, 1000, 1000, 1250, 1000, 1000, 1250, 1250, 1250, 1250])], axis=1)
        tbl_0 = 0.05 * jax.random.normal(jax.random.fold_in(_tk, 500 + 0), (1000, 16), jnp.float32)
        tbl_1 = 0.05 * jax.random.normal(jax.random.fold_in(_tk, 500 + 1), (1250, 16), jnp.float32)
        tbl_2 = 0.05 * jax.random.normal(jax.random.fold_in(_tk, 500 + 2), (125000, 16), jnp.float32)
        tbl_3 = 0.05 * jax.random.normal(jax.random.fold_in(_tk, 500 + 3), (1000, 16), jnp.float32)
        tbl_4 = 0.05 * jax.random.normal(jax.random.fold_in(_tk, 500 + 4), (12500, 16), jnp.float32)
        tbl_5 = 0.05 * jax.random.normal(jax.random.fold_in(_tk, 500 + 5), (125000, 16), jnp.float32)
        tbl_6 = 0.05 * jax.random.normal(jax.random.fold_in(_tk, 500 + 6), (1250, 16), jnp.float32)
        tbl_7 = 0.05 * jax.random.normal(jax.random.fold_in(_tk, 500 + 7), (125000, 16), jnp.float32)
        tbl_8 = 0.05 * jax.random.normal(jax.random.fold_in(_tk, 500 + 8), (125000, 16), jnp.float32)
        tbl_9 = 0.05 * jax.random.normal(jax.random.fold_in(_tk, 500 + 9), (125000, 16), jnp.float32)
        tbl_10 = 0.05 * jax.random.normal(jax.random.fold_in(_tk, 500 + 10), (12500, 16), jnp.float32)
        tbl_11 = 0.05 * jax.random.normal(jax.random.fold_in(_tk, 500 + 11), (1000, 16), jnp.float32)
        tbl_12 = 0.05 * jax.random.normal(jax.random.fold_in(_tk, 500 + 12), (125000, 16), jnp.float32)
        tbl_13 = 0.05 * jax.random.normal(jax.random.fold_in(_tk, 500 + 13), (125000, 16), jnp.float32)
        tbl_14 = 0.05 * jax.random.normal(jax.random.fold_in(_tk, 500 + 14), (125000, 16), jnp.float32)
        tbl_15 = 0.05 * jax.random.normal(jax.random.fold_in(_tk, 500 + 15), (1000, 16), jnp.float32)
        tbl_16 = 0.05 * jax.random.normal(jax.random.fold_in(_tk, 500 + 16), (12500, 16), jnp.float32)
        tbl_17 = 0.05 * jax.random.normal(jax.random.fold_in(_tk, 500 + 17), (125000, 16), jnp.float32)
        tbl_18 = 0.05 * jax.random.normal(jax.random.fold_in(_tk, 500 + 18), (1250, 16), jnp.float32)
        tbl_19 = 0.05 * jax.random.normal(jax.random.fold_in(_tk, 500 + 19), (1250, 16), jnp.float32)
        tbl_20 = 0.05 * jax.random.normal(jax.random.fold_in(_tk, 500 + 20), (1250, 16), jnp.float32)
        tbl_21 = 0.05 * jax.random.normal(jax.random.fold_in(_tk, 500 + 21), (125000, 16), jnp.float32)
        tbl_22 = 0.05 * jax.random.normal(jax.random.fold_in(_tk, 500 + 22), (1000, 16), jnp.float32)
        tbl_23 = 0.05 * jax.random.normal(jax.random.fold_in(_tk, 500 + 23), (125000, 16), jnp.float32)
        tbl_24 = 0.05 * jax.random.normal(jax.random.fold_in(_tk, 500 + 24), (125000, 16), jnp.float32)
        tbl_25 = 0.05 * jax.random.normal(jax.random.fold_in(_tk, 500 + 25), (1250, 16), jnp.float32)
        tbl_26 = 0.05 * jax.random.normal(jax.random.fold_in(_tk, 500 + 26), (125000, 16), jnp.float32)
        tbl_27 = 0.05 * jax.random.normal(jax.random.fold_in(_tk, 500 + 27), (1250, 16), jnp.float32)
        tbl_28 = 0.05 * jax.random.normal(jax.random.fold_in(_tk, 500 + 28), (1250, 16), jnp.float32)
        tbl_29 = 0.05 * jax.random.normal(jax.random.fold_in(_tk, 500 + 29), (12500, 16), jnp.float32)
        tbl_30 = 0.05 * jax.random.normal(jax.random.fold_in(_tk, 500 + 30), (12500, 16), jnp.float32)
        tbl_31 = 0.05 * jax.random.normal(jax.random.fold_in(_tk, 500 + 31), (12500, 16), jnp.float32)
        tbl_32 = 0.05 * jax.random.normal(jax.random.fold_in(_tk, 500 + 32), (12500, 16), jnp.float32)
        tbl_33 = 0.05 * jax.random.normal(jax.random.fold_in(_tk, 500 + 33), (125000, 16), jnp.float32)
        tbl_34 = 0.05 * jax.random.normal(jax.random.fold_in(_tk, 500 + 34), (12500, 16), jnp.float32)
        tbl_35 = 0.05 * jax.random.normal(jax.random.fold_in(_tk, 500 + 35), (12500, 16), jnp.float32)
        tbl_36 = 0.05 * jax.random.normal(jax.random.fold_in(_tk, 500 + 36), (1000, 16), jnp.float32)
        tbl_37 = 0.05 * jax.random.normal(jax.random.fold_in(_tk, 500 + 37), (1250, 16), jnp.float32)
        tbl_38 = 0.05 * jax.random.normal(jax.random.fold_in(_tk, 500 + 38), (1000, 16), jnp.float32)
        tbl_39 = 0.05 * jax.random.normal(jax.random.fold_in(_tk, 500 + 39), (12500, 16), jnp.float32)
        tbl_40 = 0.05 * jax.random.normal(jax.random.fold_in(_tk, 500 + 40), (1000, 16), jnp.float32)
        tbl_41 = 0.05 * jax.random.normal(jax.random.fold_in(_tk, 500 + 41), (1250, 16), jnp.float32)
        tbl_42 = 0.05 * jax.random.normal(jax.random.fold_in(_tk, 500 + 42), (1250, 16), jnp.float32)
        tbl_43 = 0.05 * jax.random.normal(jax.random.fold_in(_tk, 500 + 43), (1000, 16), jnp.float32)
        tbl_44 = 0.05 * jax.random.normal(jax.random.fold_in(_tk, 500 + 44), (1250, 16), jnp.float32)
        tbl_45 = 0.05 * jax.random.normal(jax.random.fold_in(_tk, 500 + 45), (1250, 16), jnp.float32)
        tbl_46 = 0.05 * jax.random.normal(jax.random.fold_in(_tk, 500 + 46), (12500, 16), jnp.float32)
        tbl_47 = 0.05 * jax.random.normal(jax.random.fold_in(_tk, 500 + 47), (12500, 16), jnp.float32)
        tbl_48 = 0.05 * jax.random.normal(jax.random.fold_in(_tk, 500 + 48), (1250, 16), jnp.float32)
        tbl_49 = 0.05 * jax.random.normal(jax.random.fold_in(_tk, 500 + 49), (1000, 16), jnp.float32)
        tbl_50 = 0.05 * jax.random.normal(jax.random.fold_in(_tk, 500 + 50), (1000, 16), jnp.float32)
        tbl_51 = 0.05 * jax.random.normal(jax.random.fold_in(_tk, 500 + 51), (12500, 16), jnp.float32)
        tbl_52 = 0.05 * jax.random.normal(jax.random.fold_in(_tk, 500 + 52), (12500, 16), jnp.float32)
        tbl_53 = 0.05 * jax.random.normal(jax.random.fold_in(_tk, 500 + 53), (1000, 16), jnp.float32)
        tbl_54 = 0.05 * jax.random.normal(jax.random.fold_in(_tk, 500 + 54), (1000, 16), jnp.float32)
        tbl_55 = 0.05 * jax.random.normal(jax.random.fold_in(_tk, 500 + 55), (1000, 16), jnp.float32)
        tbl_56 = 0.05 * jax.random.normal(jax.random.fold_in(_tk, 500 + 56), (1000, 16), jnp.float32)
        tbl_57 = 0.05 * jax.random.normal(jax.random.fold_in(_tk, 500 + 57), (1250, 16), jnp.float32)
        tbl_58 = 0.05 * jax.random.normal(jax.random.fold_in(_tk, 500 + 58), (1000, 16), jnp.float32)
        tbl_59 = 0.05 * jax.random.normal(jax.random.fold_in(_tk, 500 + 59), (1000, 16), jnp.float32)
        tbl_60 = 0.05 * jax.random.normal(jax.random.fold_in(_tk, 500 + 60), (1250, 16), jnp.float32)
        tbl_61 = 0.05 * jax.random.normal(jax.random.fold_in(_tk, 500 + 61), (1250, 16), jnp.float32)
        tbl_62 = 0.05 * jax.random.normal(jax.random.fold_in(_tk, 500 + 62), (1250, 16), jnp.float32)
        tbl_63 = 0.05 * jax.random.normal(jax.random.fold_in(_tk, 500 + 63), (1250, 16), jnp.float32)
        _rk = jax.random.fold_in(_tk, 7)
        W_top1 = 0.05 * jax.random.normal(jax.random.fold_in(_tk, 801), (400, 512), jnp.float32)
        W_top2 = 0.0441942 * jax.random.normal(jax.random.fold_in(_tk, 802), (512, 256), jnp.float32)
        W_top3 = 0.0625 * jax.random.normal(jax.random.fold_in(_tk, 803), (256, 1), jnp.float32)
        b_top1 = jnp.zeros((512,), jnp.float32)
        b_top2 = jnp.zeros((256,), jnp.float32)
        return (dense_ctx, ids, tbl_0, tbl_1, tbl_2, tbl_3, tbl_4, tbl_5, tbl_6, tbl_7, tbl_8, tbl_9, tbl_10, tbl_11, tbl_12, tbl_13, tbl_14, tbl_15, tbl_16, tbl_17, tbl_18, tbl_19, tbl_20, tbl_21, tbl_22, tbl_23, tbl_24, tbl_25, tbl_26, tbl_27, tbl_28, tbl_29, tbl_30, tbl_31, tbl_32, tbl_33, tbl_34, tbl_35, tbl_36, tbl_37, tbl_38, tbl_39, tbl_40, tbl_41, tbl_42, tbl_43, tbl_44, tbl_45, tbl_46, tbl_47, tbl_48, tbl_49, tbl_50, tbl_51, tbl_52, tbl_53, tbl_54, tbl_55, tbl_56, tbl_57, tbl_58, tbl_59, tbl_60, tbl_61, tbl_62, tbl_63, W_top1, b_top1, W_top2, b_top2, W_top3)
    dense_ctx, ids, tbl_0, tbl_1, tbl_2, tbl_3, tbl_4, tbl_5, tbl_6, tbl_7, tbl_8, tbl_9, tbl_10, tbl_11, tbl_12, tbl_13, tbl_14, tbl_15, tbl_16, tbl_17, tbl_18, tbl_19, tbl_20, tbl_21, tbl_22, tbl_23, tbl_24, tbl_25, tbl_26, tbl_27, tbl_28, tbl_29, tbl_30, tbl_31, tbl_32, tbl_33, tbl_34, tbl_35, tbl_36, tbl_37, tbl_38, tbl_39, tbl_40, tbl_41, tbl_42, tbl_43, tbl_44, tbl_45, tbl_46, tbl_47, tbl_48, tbl_49, tbl_50, tbl_51, tbl_52, tbl_53, tbl_54, tbl_55, tbl_56, tbl_57, tbl_58, tbl_59, tbl_60, tbl_61, tbl_62, tbl_63, W_top1, b_top1, W_top2, b_top2, W_top3 = _rec_inputs()

    def _L0_rec_setup():
        import jax, jax.numpy as jnp
        import numpy as np
        BATCH, FIELDS, EMBED = (256, 64, 16)
        LAYERS = [128, 128, 128]
        key = jax.random.key(seed)
        ks = jax.random.split(key, 7)
        inp = {'input': jax.random.normal(ks[0], (BATCH, FIELDS, EMBED), dtype=jnp.float32)}
        in_ch = [FIELDS * FIELDS, FIELDS * LAYERS[0], FIELDS * LAYERS[1]]
        for i, (cin, cout) in enumerate(zip(in_ch, LAYERS)):
            scale = 1.0 / np.sqrt(cin)
            inp[f'W{i}'] = jax.random.uniform(ks[1 + 2 * i], (cout, cin), jnp.float32, -scale, scale)
            inp[f'b{i}'] = jax.random.uniform(ks[2 + 2 * i], (cout,), jnp.float32, -scale, scale)
        return inp
    _L0_rec_all = _L0_rec_setup()
    _L0_rec_in = {k: v for k, v in _L0_rec_all.items() if k in ('W0', 'b0', 'W1', 'b1', 'W2', 'b2')}
    del _L0_rec_all
    return {'dense_ctx': dense_ctx, 'ids': ids, 'tbl_0': tbl_0, 'tbl_1': tbl_1, 'tbl_2': tbl_2, 'tbl_3': tbl_3, 'tbl_4': tbl_4, 'tbl_5': tbl_5, 'tbl_6': tbl_6, 'tbl_7': tbl_7, 'tbl_8': tbl_8, 'tbl_9': tbl_9, 'tbl_10': tbl_10, 'tbl_11': tbl_11, 'tbl_12': tbl_12, 'tbl_13': tbl_13, 'tbl_14': tbl_14, 'tbl_15': tbl_15, 'tbl_16': tbl_16, 'tbl_17': tbl_17, 'tbl_18': tbl_18, 'tbl_19': tbl_19, 'tbl_20': tbl_20, 'tbl_21': tbl_21, 'tbl_22': tbl_22, 'tbl_23': tbl_23, 'tbl_24': tbl_24, 'tbl_25': tbl_25, 'tbl_26': tbl_26, 'tbl_27': tbl_27, 'tbl_28': tbl_28, 'tbl_29': tbl_29, 'tbl_30': tbl_30, 'tbl_31': tbl_31, 'tbl_32': tbl_32, 'tbl_33': tbl_33, 'tbl_34': tbl_34, 'tbl_35': tbl_35, 'tbl_36': tbl_36, 'tbl_37': tbl_37, 'tbl_38': tbl_38, 'tbl_39': tbl_39, 'tbl_40': tbl_40, 'tbl_41': tbl_41, 'tbl_42': tbl_42, 'tbl_43': tbl_43, 'tbl_44': tbl_44, 'tbl_45': tbl_45, 'tbl_46': tbl_46, 'tbl_47': tbl_47, 'tbl_48': tbl_48, 'tbl_49': tbl_49, 'tbl_50': tbl_50, 'tbl_51': tbl_51, 'tbl_52': tbl_52, 'tbl_53': tbl_53, 'tbl_54': tbl_54, 'tbl_55': tbl_55, 'tbl_56': tbl_56, 'tbl_57': tbl_57, 'tbl_58': tbl_58, 'tbl_59': tbl_59, 'tbl_60': tbl_60, 'tbl_61': tbl_61, 'tbl_62': tbl_62, 'tbl_63': tbl_63, 'W_top1': W_top1, 'b_top1': b_top1, 'W_top2': W_top2, 'b_top2': b_top2, 'W_top3': W_top3, 'L0_rec_W0': _L0_rec_in['W0'], 'L0_rec_b0': _L0_rec_in['b0'], 'L0_rec_W1': _L0_rec_in['W1'], 'L0_rec_b1': _L0_rec_in['b1'], 'L0_rec_W2': _L0_rec_in['W2'], 'L0_rec_b2': _L0_rec_in['b2']}

def reference(dense_ctx, ids, tbl_0, tbl_1, tbl_2, tbl_3, tbl_4, tbl_5, tbl_6, tbl_7, tbl_8, tbl_9, tbl_10, tbl_11, tbl_12, tbl_13, tbl_14, tbl_15, tbl_16, tbl_17, tbl_18, tbl_19, tbl_20, tbl_21, tbl_22, tbl_23, tbl_24, tbl_25, tbl_26, tbl_27, tbl_28, tbl_29, tbl_30, tbl_31, tbl_32, tbl_33, tbl_34, tbl_35, tbl_36, tbl_37, tbl_38, tbl_39, tbl_40, tbl_41, tbl_42, tbl_43, tbl_44, tbl_45, tbl_46, tbl_47, tbl_48, tbl_49, tbl_50, tbl_51, tbl_52, tbl_53, tbl_54, tbl_55, tbl_56, tbl_57, tbl_58, tbl_59, tbl_60, tbl_61, tbl_62, tbl_63, W_top1, b_top1, W_top2, b_top2, W_top3, L0_rec_W0, L0_rec_b0, L0_rec_W1, L0_rec_b1, L0_rec_W2, L0_rec_b2):
    import jax
    import jax.numpy as jnp

    def _L0_rec_ref(input, W0, b0, W1, b1, W2, b2):
        import jax, jax.numpy as jnp
        import numpy as np
        BATCH, FIELDS, EMBED = (256, 64, 16)
        LAYERS = [128, 128, 128]
        params = [(W0, b0), (W1, b1), (W2, b2)]
        x_vec = input
        outs = []
        for W, b in params:
            z = jnp.einsum('bhd,bfd->bhfd', x_vec, input)
            B, h, f, d = z.shape
            z = z.reshape(B, h * f, d)
            x_vec = jnp.einsum('oc,bcd->bod', W, z) + b[None, :, None]
            outs.append(x_vec.sum(axis=2))
        return jnp.concatenate(outs, axis=1)
    e = jnp.stack([tbl_0[ids[:, 0]], tbl_1[ids[:, 1]], tbl_2[ids[:, 2]], tbl_3[ids[:, 3]], tbl_4[ids[:, 4]], tbl_5[ids[:, 5]], tbl_6[ids[:, 6]], tbl_7[ids[:, 7]], tbl_8[ids[:, 8]], tbl_9[ids[:, 9]], tbl_10[ids[:, 10]], tbl_11[ids[:, 11]], tbl_12[ids[:, 12]], tbl_13[ids[:, 13]], tbl_14[ids[:, 14]], tbl_15[ids[:, 15]], tbl_16[ids[:, 16]], tbl_17[ids[:, 17]], tbl_18[ids[:, 18]], tbl_19[ids[:, 19]], tbl_20[ids[:, 20]], tbl_21[ids[:, 21]], tbl_22[ids[:, 22]], tbl_23[ids[:, 23]], tbl_24[ids[:, 24]], tbl_25[ids[:, 25]], tbl_26[ids[:, 26]], tbl_27[ids[:, 27]], tbl_28[ids[:, 28]], tbl_29[ids[:, 29]], tbl_30[ids[:, 30]], tbl_31[ids[:, 31]], tbl_32[ids[:, 32]], tbl_33[ids[:, 33]], tbl_34[ids[:, 34]], tbl_35[ids[:, 35]], tbl_36[ids[:, 36]], tbl_37[ids[:, 37]], tbl_38[ids[:, 38]], tbl_39[ids[:, 39]], tbl_40[ids[:, 40]], tbl_41[ids[:, 41]], tbl_42[ids[:, 42]], tbl_43[ids[:, 43]], tbl_44[ids[:, 44]], tbl_45[ids[:, 45]], tbl_46[ids[:, 46]], tbl_47[ids[:, 47]], tbl_48[ids[:, 48]], tbl_49[ids[:, 49]], tbl_50[ids[:, 50]], tbl_51[ids[:, 51]], tbl_52[ids[:, 52]], tbl_53[ids[:, 53]], tbl_54[ids[:, 54]], tbl_55[ids[:, 55]], tbl_56[ids[:, 56]], tbl_57[ids[:, 57]], tbl_58[ids[:, 58]], tbl_59[ids[:, 59]], tbl_60[ids[:, 60]], tbl_61[ids[:, 61]], tbl_62[ids[:, 62]], tbl_63[ids[:, 63]]], axis=1)
    z = _L0_rec_ref(e, L0_rec_W0, L0_rec_b0, L0_rec_W1, L0_rec_b1, L0_rec_W2, L0_rec_b2)
    z = z.reshape(z.shape[0], -1)
    h = jnp.concatenate([z, dense_ctx], axis=1)
    h = jnp.maximum(h @ W_top1 + b_top1, 0.0)
    h = jnp.maximum(h @ W_top2 + b_top2, 0.0)
    y = h @ W_top3
    return y

_drawn_inputs = setup_inputs


def setup_inputs(seed=0):
    import zlib

    import numpy as np

    out = dict(_drawn_inputs(seed))
    spreads = {'b_top1': (0.0, 0.1), 'b_top2': (0.0, 0.1)}
    factors = {'tbl_0': 8.0,
     'tbl_1': 8.0,
     'tbl_2': 8.0,
     'tbl_3': 8.0,
     'tbl_4': 8.0,
     'tbl_5': 8.0,
     'tbl_6': 8.0,
     'tbl_7': 8.0,
     'tbl_8': 8.0,
     'tbl_9': 8.0,
     'tbl_10': 8.0,
     'tbl_11': 8.0,
     'tbl_12': 8.0,
     'tbl_13': 8.0,
     'tbl_14': 8.0,
     'tbl_15': 8.0,
     'tbl_16': 8.0,
     'tbl_17': 8.0,
     'tbl_18': 8.0,
     'tbl_19': 8.0,
     'tbl_20': 8.0,
     'tbl_21': 8.0,
     'tbl_22': 8.0,
     'tbl_23': 8.0,
     'tbl_24': 8.0,
     'tbl_25': 8.0,
     'tbl_26': 8.0,
     'tbl_27': 8.0,
     'tbl_28': 8.0,
     'tbl_29': 8.0,
     'tbl_30': 8.0,
     'tbl_31': 8.0,
     'tbl_32': 8.0,
     'tbl_33': 8.0,
     'tbl_34': 8.0,
     'tbl_35': 8.0,
     'tbl_36': 8.0,
     'tbl_37': 8.0,
     'tbl_38': 8.0,
     'tbl_39': 8.0,
     'tbl_40': 8.0,
     'tbl_41': 8.0,
     'tbl_42': 8.0,
     'tbl_43': 8.0,
     'tbl_44': 8.0,
     'tbl_45': 8.0,
     'tbl_46': 8.0,
     'tbl_47': 8.0,
     'tbl_48': 8.0,
     'tbl_49': 8.0,
     'tbl_50': 8.0,
     'tbl_51': 8.0,
     'tbl_52': 8.0,
     'tbl_53': 8.0,
     'tbl_54': 8.0,
     'tbl_55': 8.0,
     'tbl_56': 8.0,
     'tbl_57': 8.0,
     'tbl_58': 8.0,
     'tbl_59': 8.0,
     'tbl_60': 8.0,
     'tbl_61': 8.0,
     'tbl_62': 8.0,
     'tbl_63': 8.0,
     'L0_rec_W1': 8.0,
     'L0_rec_W2': 8.0}
    for name, (base, spread) in spreads.items():
        noise = np.random.default_rng([zlib.crc32(name.encode()), seed]).standard_normal(out[name].shape)
        drawn = base * np.exp(spread * noise) if base else spread * noise
        out[name] = jnp.asarray(drawn.astype(out[name].dtype))
    for name, factor in factors.items():
        out[name] = (out[name] * factor).astype(out[name].dtype)
    return out
```

```python
from contextlib import ExitStack

import numpy as np

import concourse.bass as bass
from concourse import mybir

F32 = mybir.dt.float32
I32 = mybir.dt.int32
U32 = mybir.dt.uint32
ALU = mybir.AluOpType
ACT = mybir.ActivationFunctionType
AX = mybir.AxisListType

P = 128
BATCH, FIELDS, EMBED, HID, DENSE = 512, 64, 16, 128, 16
COLS = 512
CHUNK_B = COLS // EMBED
CHUNKS = BATCH // CHUNK_B
HALF_B = CHUNK_B // 2
SHIFTS = 8
PAIR_SHIFTS = 4
QUAD = 4
Z_SLOTS = 4
LAND_SLOTS = 4
GROUP_B = P // EMBED
GROUPS = CHUNK_B // GROUP_B
X0_ROWS = 3 * FIELDS
X1_ROWS = HID + SHIFTS
L1_UNITS = PAIR_SHIFTS
L2_UNITS = SHIFTS * SHIFTS // QUAD
UNITS = L1_UNITS + L2_UNITS
COPIES = PAIR_SHIFTS + SHIFTS
F_BLOCK = 16
TOP1, TOP2 = 512, 256


class Chunk:

    def __init__(self, n, r):
        self.n, self.r = n, r
        self.par = r % 2

    def plus(self, k):
        return Chunk(self.n, self.r + k)

    def count(self, per_chunk, more=0):
        if isinstance(self.n, int):
            return per_chunk * (2 * self.n + self.r) + more
        return self.n * (2 * per_chunk) + (per_chunk * self.r + more)

    def turn(self, per_turn, more=0):
        if isinstance(self.n, int):
            return per_turn * (self.n + self.r // 2) + more
        return self.n * per_turn + (per_turn * (self.r // 2) + more)


def build(nc, ids, field_info, tables, dense, w0a, w0b, w1, w2, bias, wt1, wt1d, bt1, wt2, bt2, wt3, ident, mask, out):
    x0_scratch = nc.dram_tensor("x0_scratch", (CHUNKS, X0_ROWS, COLS), F32, kind="Internal").ap()
    x1_scratch = nc.dram_tensor("x1_scratch", (CHUNKS, X1_ROWS, COLS), F32, kind="Internal").ap()
    gram_scratch = nc.dram_tensor("gram_scratch", (HID, CHUNKS, FIELDS, CHUNK_B), F32, kind="Internal").ap()

    with ExitStack() as ctx:
        def sb(name, shape, dt=F32):
            return ctx.enter_context(nc.sbuf_tensor(name, shape, dt))

        def ps(name, shape):
            return ctx.enter_context(nc.psum_tensor(name, shape, F32))

        def sem(name):
            return ctx.enter_context(nc.semaphore(name))

        ids_sb = sb("ids_sb", [P, CHUNKS * HALF_B], I32)
        ids_tmp = sb("ids_tmp", [P, CHUNKS * HALF_B])
        rows_f = sb("rows_f", [P, CHUNKS * HALF_B])
        rows = sb("rows", [P, CHUNKS * HALF_B], I32)
        rows_chunk = sb("rows_chunk", [P, 2, HALF_B], I32)
        info_sb = sb("info_sb", [P, 3])
        bias_sb = sb("bias_sb", [P, 3])
        bias3_sb = sb("bias3_sb", [P, 1])
        w0_sb = sb("w0_sb", [P, 17, HID])
        w1_sb = sb("w1_sb", [P, SHIFTS * SHIFTS, HID])
        w2_sb = sb("w2_sb", [P, FIELDS, HID])
        wt1_sb = sb("wt1_sb", [P, 3, TOP1])
        wt1d_sb = sb("wt1d_sb", [DENSE, TOP1])
        wt2_sb = sb("wt2_sb", [P, TOP1 // P, TOP2])
        wt3_sb = sb("wt3_sb", [P, TOP2 // P])
        bt1_sb = sb("bt1_sb", [P, TOP1 // P])
        bt2_sb = sb("bt2_sb", [P, TOP2 // P])
        dense_sb = sb("dense_sb", [DENSE, BATCH])
        ident_sb = sb("ident_sb", [P, P])
        mask_sb = sb("mask_sb", [P, GROUP_B])
        emb = sb("emb", [P, 2, HALF_B * EMBED])
        x0_shift = sb("x0_shift", [P, 2, SHIFTS, COLS])
        x0_pair = sb("x0_pair", [P, PAIR_SHIFTS, COLS])
        land = sb("land", [P, LAND_SLOTS, COLS])
        z = sb("z", [P, Z_SLOTS, QUAD, COLS])
        z_sq = sb("z_sq", [FIELDS, COLS])
        x1 = sb("x1", [P, COLS])
        x2 = sb("x2", [P, COLS])
        x2t = sb("x2t", [P, COLS])
        blocks = sb("blocks", [P, 2, GROUP_B, FIELDS])
        gram = sb("gram", [P, FIELDS, CHUNK_B])
        sums = sb("sums", [P, 3, BATCH])
        y_sb = sb("y_sb", [1, BATCH])

        acc1 = ps("acc1", [P, COLS])
        acc2 = [ps("acc2_even", [P, COLS]), ps("acc2_odd", [P, COLS])]
        operand = [ps("operand_even", [P, COLS]), ps("operand_odd", [P, COLS])]
        x2t_ps = ps("x2t_ps", [P, COLS])
        x0t_ps = ps("x0t_ps", [P, GROUPS, FIELDS])
        gram_ps = ps("gram_ps", [P, GROUP_B, FIELDS])

        ids_in, const_in, w0_in, w1_in, w2_in, top_in = (sem(s) for s in ("ids_in", "const_in", "w0_in", "w1_in", "w2_in", "top_in"))
        rows_step, rows_ready, rows_copied, gather_begun = (sem(s) for s in ("rows_step", "rows_ready", "rows_copied", "gather_begun"))
        w0_summed = sem("w0_summed")
        gathered = [sem("gathered_even"), sem("gathered_odd")]
        x0_stored = [sem("x0_stored_even"), sem("x0_stored_odd")]
        x0_loaded = [sem("x0_loaded_even"), sem("x0_loaded_odd")]
        pair_loaded, x1_stored, gram_stored = sem("pair_loaded"), sem("x1_stored"), sem("gram_stored")
        shift_landed = [sem(f"shift_landed_{s}") for s in range(LAND_SLOTS)]
        copied, squared = sem("copied"), sem("squared")
        formed, used = sem("formed"), sem("used")
        x2_turned, x0_turned, gram_done = (sem(s) for s in ("x2_turned", "x0_turned", "gram_done"))
        x1_ready, x2_ready, x2t_ready, gram_staged = (sem(s) for s in ("x1_ready", "x2_ready", "x2t_ready", "gram_staged"))
        sum1_ready, sum2_ready, sum3_ready, block_ready = (sem(s) for s in ("sum1_ready", "sum2_ready", "sum3_ready", "block_ready"))
        bias3_ready = sem("bias3_ready")
        gram_loaded = [sem(f"gram_loaded_{s}") for s in range(4)]
        gram_used, sp_passed = sem("gram_used"), sem("sp_passed")
        top1_done, top2_done, top3_done = sem("top1_done"), sem("top2_done"), sem("top3_done")
        h1_ready, h2_ready, y_ready, y_stored = sem("h1_ready"), sem("h2_ready"), sem("y_ready"), sem("y_stored")

        def unit(c, k):
            return c.count(UNITS, L1_UNITS + k)

        def copy(c, k):
            return c.count(COPIES, PAIR_SHIFTS + k)

        ALL_UNITS = CHUNKS * UNITS

        def layer1_used(c):
            return unit(c.plus(-1), 8 + L1_UNITS)

        gram_buffers = [x0_shift[:, 0], x0_shift[:, 1],
                        z[:, 0:2].rearrange("p a q n -> p (a q) n"), z[:, 2:4].rearrange("p a q n -> p (a q) n")]
        gram_buffers = [g.rearrange("p c (f b) -> p c f b", f=F_BLOCK) for g in gram_buffers]
        F_BLOCKS = FIELDS // F_BLOCK
        GRAM_LOADS = 2 * F_BLOCKS
        h1, h2 = land, x0_pair

        block = ctx.enter_context(nc.Block())

        @block.sync
        def _(sp):
            def at(*offsets):
                return [x if isinstance(x, int) else sp.compute_val(x) for x in offsets]

            def wait_all(*waits):
                for s, value in [(s, at(value)[0]) for s, value in waits]:
                    sp.wait_ge(s, value)
                sp.sem_inc(sp_passed, 1)

            sp.dma_start(ids_sb[:, :], ids).then_inc(ids_in, 16)
            sp.dma_start(info_sb[:, :], field_info).then_inc(ids_in, 16)
            for t, s in ((bias_sb, bias), (ident_sb, ident), (mask_sb, mask)):
                sp.dma_start(t[:, :], s).then_inc(const_in, 16)
            sp.dma_start(w0_sb[:, :, :], w0a).then_inc(w0_in, 16)
            sp.dma_start(z[:, 0:2].rearrange("p a q n -> p (a q n)")[:, 0:17 * HID], w0b).then_inc(w0_in, 16)
            sp.dma_start(w1_sb[:, :, :], w1).then_inc(w1_in, 16)

            def store_x0(c):
                offsets = at(*(c.count(X0_ROWS * COLS, s * (COLS // 2)) for s in range(2)))
                wait_all((gathered[c.par], c.turn(16 * HALF_B, 16 * HALF_B)))
                for s in range(2):
                    src = emb[s * FIELDS:(s + 1) * FIELDS, c.par, :].rearrange("p (r n) -> p r n", r=1)
                    dst = bass.AP(x0_scratch.tensor, offsets[s],
                                  [[COLS, FIELDS], [FIELDS * COLS, 3], [1, COLS // 2]])
                    sp.dma_start(dst, src.to_broadcast([FIELDS, 3, COLS // 2])).then_inc(x0_stored[c.par], 16)

            def load_x0(c, first=False):
                offset, = at(c.count(X0_ROWS * COLS))
                stored = (x0_stored[c.par], c.turn(32, 32))
                if first:
                    wait_all(stored)
                else:
                    wait_all(stored,
                             (formed, unit(c.plus(-1), 0)),
                             (x0_turned, c.count(1, -1)))
                sp.dma_start(x0_shift[:, c.par], bass.AP(
                    x0_scratch.tensor, offset,
                    [[COLS, P], [SHIFTS * COLS, SHIFTS], [1, COLS]])).then_inc(x0_loaded[c.par], 16)

            def load_pairs(c, waits):
                offsets = at(*(c.count(X0_ROWS * COLS, s * PAIR_SHIFTS * COLS) for s in range(2)))
                wait_all(*waits)
                for s in range(2):
                    sp.dma_start(x0_pair[s * FIELDS:(s + 1) * FIELDS], bass.AP(
                        x0_scratch.tensor, offsets[s],
                        [[COLS, FIELDS], [COLS, PAIR_SHIFTS], [1, COLS]])).then_inc(pair_loaded, 16)

            def store_x1(c):
                offsets = at(c.count(X1_ROWS * COLS), c.count(X1_ROWS * COLS, HID * COLS))
                wait_all((x1_ready, c.count(1, 1)))
                for offset, n in zip(offsets, (HID, SHIFTS)):
                    sp.dma_start(bass.AP(x1_scratch.tensor, offset, [[COLS, n], [1, COLS]]),
                                 x1[0:n, :]).then_inc(x1_stored, 16)

            def load_shift(c, i, *waits):
                offset, = at(c.count(X1_ROWS * COLS, i * COLS))
                wait_all(*waits)
                sp.dma_start(land[:, i % LAND_SLOTS, :], bass.AP(
                    x1_scratch.tensor, offset,
                    [[COLS, P], [1, COLS]])).then_inc(shift_landed[i % LAND_SLOTS], 16)

            def round_(c, first=False, last=False, near_end=False):
                nxt = c.plus(1)
                if not last:
                    load_x0(nxt, first=first)
                    load_pairs(nxt, [(copied, PAIR_SHIFTS if first else copy(c.plus(-1), 8)), (squared, c.count(1, 1))])
                for i in range(4, SHIFTS):
                    load_shift(c, i, (copied, copy(c, i - 3)))
                if not (last or near_end):
                    store_x0(c.plus(2))
                if not first:
                    store_gram(c.plus(-1))
                if not last:
                    store_x1(nxt)
                    for i in range(4):
                        load_shift(nxt, i, (x1_stored, nxt.count(32, 32)),
                                   (copied, copy(c, 9 + i)))

            def store_gram(c):
                offset, = at(c.count(FIELDS * CHUNK_B))
                wait_all((gram_staged, c.count(GROUPS, GROUPS)))
                sp.dma_start(bass.AP(gram_scratch.tensor, offset,
                                     [[CHUNKS * FIELDS * CHUNK_B, HID], [1, FIELDS * CHUNK_B]]),
                             gram[:, :, :].rearrange("p f b -> p (f b)")).then_inc(gram_stored, 16)

            c0 = Chunk(0, 0)
            store_x0(c0)
            load_x0(c0, first=True)
            load_pairs(c0, [])
            sp.dma_start(w2_sb[:, :, :], w2).then_inc(w2_in, 16)
            for t, s in ((wt1_sb[:, :, :], wt1), (wt1d_sb[:, :], wt1d), (bt1_sb[:, :], bt1), (wt2_sb[:, :, :], wt2),
                         (bt2_sb[:, :], bt2), (wt3_sb[:, :], wt3), (dense_sb[:, :], dense)):
                sp.dma_start(t, s).then_inc(top_in, 16)
            store_x0(c0.plus(1))
            store_x1(c0)
            sp.wait_ge(x1_stored, 32)
            for i in range(4):
                load_shift(c0, i)
            round_(c0, first=True)
            with sp.Fori(0, (CHUNKS - 4) // 2) as n:
                round_(Chunk(n, 1))
                round_(Chunk(n, 2))
            round_(Chunk(0, CHUNKS - 3))
            round_(Chunk(0, CHUNKS - 2), near_end=True)
            round_(Chunk(0, CHUNKS - 1), last=True)

            def load_gram(k):
                half, fb = k // F_BLOCKS, k % F_BLOCKS
                sp.dma_start(gram_buffers[k % 4].rearrange("p c f b -> p c (f b)"), bass.AP(
                    gram_scratch.tensor, (half * (CHUNKS // 2) * FIELDS + fb * F_BLOCK) * CHUNK_B,
                    [[CHUNKS * FIELDS * CHUNK_B, HID], [FIELDS * CHUNK_B, CHUNKS // 2], [1, F_BLOCK * CHUNK_B]],
                )).then_inc(gram_loaded[k % 4], 16)

            sp.wait_ge(gram_stored, 16 * (CHUNKS - 1))
            sp.wait_ge(x0_turned, CHUNKS - 1)
            load_gram(0)
            sp.wait_ge(formed, ALL_UNITS)
            sp.wait_ge(x0_turned, CHUNKS)
            load_gram(1)
            sp.wait_ge(used, ALL_UNITS)
            load_gram(2)
            load_gram(3)
            store_gram(Chunk(0, CHUNKS - 1))
            sp.wait_ge(gram_stored, 16 * CHUNKS)
            for k in range(4, GRAM_LOADS):
                sp.wait_ge(gram_used, k - 3)
                load_gram(k)
            sp.wait_ge(y_ready, 1)
            sp.dma_start(out.rearrange("b o -> o b"), y_sb[:, :]).then_inc(y_stored, 16)
            sp.wait_ge(y_stored, 16)
            for par in range(2):
                sp.wait_ge(x0_stored[par], 16 * CHUNKS)
            sp.wait_ge(x1_stored, 32 * CHUNKS)

        @block.gpsimd
        def _(pool):
            def gather(c, first=False):
                if not first:
                    pool.wait_ge(x0_stored[c.par], c.turn(32))
                pool.tensor_copy(rows_chunk[:, c.par, :], rows[:, bass.ds(c.count(HALF_B), HALF_B)]).then_inc(rows_copied, 1)
                pool.wait_ge(rows_copied, c.count(1, 1))
                pool.sem_inc(gather_begun, 1)
                for j in range(HALF_B):
                    pool.indirect_dma_start(
                        out=emb[:, c.par, j * EMBED:(j + 1) * EMBED], out_offset=None, in_=tables,
                        in_offset=bass.IndirectOffsetOnAxis(ap=rows_chunk[:, c.par, j:j + 1], axis=0),
                    ).then_inc(gathered[c.par], 16)

            pool.wait_ge(rows_ready, 1)
            gather(Chunk(0, 0), first=True)
            gather(Chunk(0, 1), first=True)
            with pool.Fori(0, (CHUNKS - 2) // 2) as n:
                gather(Chunk(n, 2))
                gather(Chunk(n, 3))

        @block.vector
        def _(dve):
            dve.wait_ge(ids_in, 32)
            dve.tensor_scalar(ids_tmp[:, :], ids_sb[:, :], 0.0, info_sb[:, 0:1], ALU.is_lt, ALU.mult).then_inc(rows_step, 1)
            dve.wait_ge(rows_step, 1)
            dve.tensor_tensor(rows_f[:, :], ids_tmp[:, :], ids_sb[:, :], ALU.add).then_inc(rows_step, 1)
            dve.wait_ge(rows_step, 2)
            dve.tensor_scalar(ids_tmp[:, :], rows_f[:, :], 0.0, info_sb[:, 1:2], ALU.max, ALU.min).then_inc(rows_step, 1)
            dve.wait_ge(rows_step, 3)
            dve.tensor_scalar(rows[:, :], ids_tmp[:, :], info_sb[:, 2:3], None, ALU.add).then_inc(rows_ready, 1)
            dve.wait_ge(w0_in, 32)
            w0_flat = w0_sb[:, :, :].rearrange("p t o -> p (t o)")
            dve.tensor_tensor(w0_flat, w0_flat, z[:, 0:2].rearrange("p a q n -> p (a q n)")[:, 0:17 * HID],
                              ALU.add).then_inc(w0_summed, 1)
            dve.wait_ge(w0_summed, 1)
            dve.wait_ge(const_in, 48)
            dve.tensor_scalar(bias3_sb[:, :], bias_sb[:, 2:3], float(EMBED), None, ALU.mult).then_inc(bias3_ready, 1)

            def form(slot, bank, x0_tiles, c_unit, first=False):
                if not first:
                    dve.wait_ge(used, c_unit)
                dve.tensor_tensor(z[:, slot], operand[bank][:, :].rearrange("p (q n) -> p q n", q=1)
                                  .to_broadcast([P, QUAD, COLS]), x0_tiles, ALU.mult).then_inc(formed, 1)

            def form_layer1(c, m, before, first=False):
                dve.wait_ge(copied, before(m))
                if m == 0:
                    dve.wait_ge(x0_loaded[c.par], c.turn(16, 16))
                form(m % Z_SLOTS, m % 2, x0_shift[:, c.par, 1:5], None if first else unit(c.plus(-1), 8 + m - 3), first)

            def form_layer2(c, k, late=L1_UNITS):
                i, q = k // 2, k % 2
                place = k if k < 8 else k + late
                if q == 0:
                    dve.wait_ge(copied, copy(c, (i if i < 4 else i + late) + 1))
                form(place % Z_SLOTS, i % 2, x0_shift[:, c.par, 4 * q:4 * q + 4], unit(c, place - 3))

            def form_block(c, g, wait_used):
                if g == 0:
                    dve.wait_ge(x0_turned, c.count(1, 1))
                if wait_used:
                    dve.wait_ge(gram_done, c.count(GROUPS, g - 1))
                dve.tensor_tensor(
                    blocks[:, g % 2], x0t_ps[:, g:g + 1, :].to_broadcast([P, GROUP_B, FIELDS]),
                    mask_sb[:, :].rearrange("p (b f) -> p b f", f=1).to_broadcast([P, GROUP_B, FIELDS]),
                    ALU.mult).then_inc(block_ready, 1)

            def sum1(c):
                dve.wait_ge(x1_ready, c.count(1, 1))
                dve.tensor_reduce(sums[:, 0, bass.ds(c.count(CHUNK_B), CHUNK_B)],
                                  x1[:, :].rearrange("p (b d) -> p b d", d=EMBED), AX.X, ALU.add).then_inc(sum1_ready, 1)

            def sum2(c):
                dve.wait_ge(x2_ready, c.count(1, 1))
                dve.tensor_reduce(sums[:, 1, bass.ds(c.count(CHUNK_B), CHUNK_B)],
                                  x2[:, :].rearrange("p (b d) -> p b d", d=EMBED), AX.X, ALU.add).then_inc(sum2_ready, 1)

            def round_(c, first=False, second=False, last=False):
                prev, nxt = c.plus(-1), c.plus(1)
                for k in range(4):
                    form_layer2(c, k)
                if not first:
                    form_block(prev, 0, not second)
                    form_block(prev, 1, not second)
                sum1(c)
                form_layer2(c, 4)
                form_layer2(c, 5)
                if not first:
                    sum2(prev)
                form_layer2(c, 6)
                if not first:
                    form_block(prev, 2, True)
                form_layer2(c, 7)
                if not first:
                    form_block(prev, 3, True)
                if not last:
                    for m in range(PAIR_SHIFTS):
                        form_layer1(nxt, m, lambda m: copy(c, 5 + m))
                for k in range(8, 16):
                    form_layer2(c, k, 0 if last else L1_UNITS)

            c0 = Chunk(0, 0)
            for m in range(PAIR_SHIFTS):
                form_layer1(c0, m, lambda m: m + 1, first=True)
            round_(c0, first=True)
            round_(c0.plus(1), second=True)
            round_(c0.plus(2))
            with dve.Fori(0, (CHUNKS - 4) // 2) as n:
                round_(Chunk(n, 3))
                round_(Chunk(n, 4))
            round_(Chunk(0, CHUNKS - 1), last=True)
            end = Chunk(0, CHUNKS - 1)
            for g in range(GROUPS):
                form_block(end, g, True)
            sum2(end)

        @block.scalar
        def _(act):
            def to_bank(src, k, formed_before, landed=None):
                if landed is not None:
                    act.wait_ge(*landed)
                if formed_before is not None:
                    act.wait_ge(formed, formed_before)
                act.activation(operand[k % 2][:, :], src, ACT.Copy).then_inc(copied, 1)

            def shift_to_bank(c, i, formed_before):
                to_bank(land[:, i % LAND_SLOTS, :], i, formed_before,
                        (shift_landed[i % LAND_SLOTS], c.count(32, 16 * (i // 4 + 1))))

            def pair_to_bank(c, m, formed_before):
                if m == 0:
                    act.wait_ge(pair_loaded, c.count(32, 32))
                to_bank(x0_pair[:, m, :], m, formed_before)

            def square(c, first=False, second=False):
                if not first:
                    act.wait_ge(used, layer1_used(c.plus(-1)) if not second else L1_UNITS)
                act.activation(z_sq[:, :], x0_pair[0:FIELDS, 0, :], ACT.Square).then_inc(squared, 1)

            def take_x1(c, first=False):
                act.wait_ge(used, L1_UNITS if first else layer1_used(c))
                if not first:
                    act.wait_ge(x1_stored, c.count(32))
                    act.wait_ge(sum1_ready, c.count(1))
                act.activation(x1[:, :], acc1[:, :], ACT.Identity, bias=bias_sb[:, 0:1]).then_inc(x1_ready, 1)

            def take_x2(c, first=False, last=False):
                act.wait_ge(used, ALL_UNITS if last else unit(c, UNITS))
                if not first:
                    act.wait_ge(sum2_ready, c.count(1))
                    act.wait_ge(x2_turned, c.count(1))
                act.activation(x2[:, :], acc2[c.par][:, :], ACT.Identity, bias=bias_sb[:, 1:2]).then_inc(x2_ready, 1)

            def take_x2t(c, first=False):
                act.wait_ge(x2_turned, c.count(1, 1))
                if not first:
                    act.wait_ge(gram_done, c.count(GROUPS))
                act.activation(x2t[:, :], x2t_ps[:, :], ACT.Copy).then_inc(x2t_ready, 1)

            def take_gram(c, g, first=False):
                act.wait_ge(gram_done, c.count(GROUPS, g + 1))
                if g == 0 and not first:
                    act.wait_ge(gram_stored, c.count(16))
                act.activation(gram[:, :, g * GROUP_B:(g + 1) * GROUP_B].rearrange("p f b -> p b f"),
                               gram_ps[:, :, :], ACT.Copy).then_inc(gram_staged, 1)

            def round_(c, first=False, second=False, last=False):
                prev, nxt = c.plus(-1), c.plus(1)
                if not first:
                    take_x2(prev, first=second)
                shift_to_bank(c, 2, unit(c, 2))
                if not first:
                    take_x2t(prev, first=second)
                shift_to_bank(c, 3, unit(c, 4))
                if not first:
                    take_gram(prev, 0, first=second)
                if not last:
                    pair_to_bank(nxt, 0, unit(c, 6))
                if not first:
                    take_gram(prev, 1)
                if not last:
                    pair_to_bank(nxt, 1, unit(c, 8))
                if not first:
                    take_gram(prev, 2)
                    take_gram(prev, 3)
                if last:
                    for i in range(4, SHIFTS):
                        shift_to_bank(c, i, unit(c, 2 * i - 2))
                    return
                square(nxt, second=first)
                pair_to_bank(nxt, 2, unit(c, 9))
                pair_to_bank(nxt, 3, unit(c, 10))
                shift_to_bank(c, 4, unit(c, 11))
                shift_to_bank(c, 5, unit(c, 12))
                take_x1(nxt)
                shift_to_bank(c, 6, unit(c, 14))
                shift_to_bank(c, 7, unit(c, 16))
                shift_to_bank(nxt, 0, unit(c, 18))
                shift_to_bank(nxt, 1, unit(c, 20))

            c0 = Chunk(0, 0)
            pair_to_bank(c0, 0, None)
            pair_to_bank(c0, 1, None)
            square(c0, first=True)
            pair_to_bank(c0, 2, 1)
            pair_to_bank(c0, 3, 2)
            act.wait_ge(const_in, 48)
            take_x1(c0, first=True)
            shift_to_bank(c0, 0, 3)
            shift_to_bank(c0, 1, 4)
            round_(c0, first=True)
            round_(c0.plus(1), second=True)
            round_(c0.plus(2))
            with act.Fori(0, (CHUNKS - 4) // 2) as n:
                round_(Chunk(n, 3))
                round_(Chunk(n, 4))
            end = Chunk(0, CHUNKS - 1)
            round_(end, last=True)
            take_x2(end, last=True)
            take_x2t(end)
            for g in range(GROUPS):
                take_gram(end, g)
            act.wait_ge(gram_used, GRAM_LOADS)
            act.wait_ge(bias3_ready, 1)
            act.activation(sums[:, 2, :], acc2[0][:, :], ACT.Identity, bias=bias3_sb[:, 0:1]).then_inc(sum3_ready, 1)
            act.wait_ge(top_in, 7 * 16)
            act.wait_ge(copied, CHUNKS * COPIES)
            for m, bank in enumerate((acc1, operand[0], operand[1], acc2[1])):
                act.wait_ge(top1_done, m + 1)
                act.activation(h1[:, m, :], bank[:, :], ACT.Relu, bias=bt1_sb[:, m:m + 1]).then_inc(h1_ready, 1)
            for m, bank in enumerate((x2t_ps[:, :], gram_ps[:, :, :].rearrange("p b f -> p (b f)"))):
                act.wait_ge(top2_done, m + 1)
                act.activation(h2[:, m, :], bank, ACT.Relu, bias=bt2_sb[:, m:m + 1]).then_inc(h2_ready, 1)
            act.wait_ge(top3_done, 1)
            act.activation(y_sb[:, :], acc2[0][0:1, :], ACT.Copy).then_inc(y_ready, 1)

        @block.tensor
        def _(pe):
            def use(c_unit, slot, w, tile0, acc, start, stop):
                pe.wait_ge(formed, c_unit)
                for q in range(QUAD):
                    mm = pe.matmul(acc[:, :], w[:, tile0 + q, :], z[:, slot, q, :],
                                   start=start and q == 0, stop=stop and q == QUAD - 1)
                mm.then_inc(used, 1)

            def layer1(c, before, first=False):
                pe.wait_ge(squared, c.count(1, 1))
                if not first:
                    pe.wait_ge(x1_ready, c.count(1))
                pe.matmul(acc1[:, :], w0_sb[0:FIELDS, 16, :], z_sq[:, :], start=True, stop=False)
                for m in range(PAIR_SHIFTS):
                    use(before(m), m, w0_sb, m * QUAD, acc1, False, m == PAIR_SHIFTS - 1)

            def layer2(c, k, late_shift=L1_UNITS):
                place = k if k < 8 else k + late_shift
                use(unit(c, place + 1), place % Z_SLOTS, w1_sb, k * QUAD, acc2[c.par], k == 0, k == 15)

            def turn_x2(c, first=False):
                pe.wait_ge(x2_ready, c.count(1, 1))
                if not first:
                    pe.wait_ge(x2t_ready, c.count(1))
                for g in range(GROUPS):
                    t = pe.transpose(x2t_ps[:, g * P:(g + 1) * P], x2[:, g * P:(g + 1) * P], ident_sb[:, :])
                t.then_inc(x2_turned, 1)

            def turn_x0(c):
                for g in range(GROUPS):
                    t = pe.transpose(x0t_ps[:, g, :], x0_shift[0:FIELDS, c.par, 0, g * P:(g + 1) * P],
                                     ident_sb[0:FIELDS, 0:FIELDS])
                t.then_inc(x0_turned, 1)

            def gram_of(c, g, first=False):
                if g == 0:
                    pe.wait_ge(x2t_ready, c.count(1, 1))
                pe.wait_ge(block_ready, c.count(GROUPS, g + 1))
                if not first:
                    pe.wait_ge(gram_staged, c.count(GROUPS, g))
                pe.matmul(gram_ps[:, :, :].rearrange("p b f -> p (b f)"), x2t[:, g * P:(g + 1) * P],
                          blocks[:, g % 2].rearrange("p b f -> p (b f)"), start=True, stop=True).then_inc(gram_done, 1)

            def round_(c, first=False, second=False, last=False):
                prev, nxt = c.plus(-1), c.plus(1)
                layer2(c, 0)
                layer2(c, 1)
                if not first:
                    turn_x2(prev, first=second)
                layer2(c, 2)
                layer2(c, 3)
                if not first:
                    gram_of(prev, 0, first=second)
                layer2(c, 4)
                if not first:
                    gram_of(prev, 1)
                layer2(c, 5)
                layer2(c, 6)
                if not first:
                    gram_of(prev, 2)
                layer2(c, 7)
                if not first:
                    gram_of(prev, 3)
                if not last:
                    layer1(nxt, lambda m: unit(c, 8 + m + 1))
                late = 0 if last else L1_UNITS
                for k in range(8, 11):
                    layer2(c, k, late)
                if not first:
                    pe.wait_ge(block_ready, c.count(GROUPS))
                layer2(c, 11, late)
                turn_x0(c)
                for k in range(12, 16):
                    layer2(c, k, late)

            c0 = Chunk(0, 0)
            pe.wait_ge(w0_summed, 1)
            layer1(c0, lambda m: m + 1, first=True)
            pe.wait_ge(w1_in, 16)
            pe.wait_ge(const_in, 48)
            round_(c0, first=True)
            round_(c0.plus(1), second=True)
            round_(c0.plus(2))
            with pe.Fori(0, (CHUNKS - 4) // 2) as n:
                round_(Chunk(n, 3))
                round_(Chunk(n, 4))
            end = Chunk(0, CHUNKS - 1)
            round_(end, last=True)

            top_banks = (acc1, operand[0], operand[1], acc2[1])

            def top1_begin(m):
                pe.matmul(top_banks[m][:, :], wt1d_sb[:, m * P:(m + 1) * P], dense_sb[:, :], start=True, stop=False)
                pe.matmul(top_banks[m][:, :], wt1_sb[:, 0, m * P:(m + 1) * P], sums[:, 0, :], start=False, stop=False)

            turn_x2(end)
            pe.wait_ge(top_in, 7 * 16)
            pe.wait_ge(sum1_ready, CHUNKS)
            pe.wait_ge(formed, ALL_UNITS)
            for g in range(GROUPS):
                top1_begin(g)
                gram_of(end, g)
            pe.wait_ge(sum2_ready, CHUNKS)
            for m in range(TOP1 // P):
                pe.matmul(top_banks[m][:, :], wt1_sb[:, 1, m * P:(m + 1) * P], sums[:, 1, :], start=False, stop=False)

            pe.wait_ge(w2_in, 16)
            half_b = BATCH // 2
            for k in range(GRAM_LOADS):
                half, fb = k // F_BLOCKS, k % F_BLOCKS
                pe.wait_ge(gram_loaded[k % 4], 16 * (k // 4 + 1))
                for f in range(F_BLOCK):
                    ff = fb * F_BLOCK + f
                    mm = pe.matmul(acc2[0][:, half * half_b:(half + 1) * half_b], w2_sb[:, ff, :],
                                   gram_buffers[k % 4][:, :, f, :], start=ff == 0, stop=ff == FIELDS - 1)
                mm.then_inc(gram_used, 1)

            pe.wait_ge(sum3_ready, 1)
            for m in range(TOP1 // P):
                pe.matmul(top_banks[m][:, :], wt1_sb[:, 2, m * P:(m + 1) * P], sums[:, 2, :],
                          start=False, stop=True).then_inc(top1_done, 1)
            for m, bank in enumerate((x2t_ps[:, :], gram_ps[:, :, :].rearrange("p b f -> p (b f)"))):
                for k in range(TOP1 // P):
                    if m == 0:
                        pe.wait_ge(h1_ready, k + 1)
                    mm = pe.matmul(bank, wt2_sb[:, k, m * P:(m + 1) * P], h1[:, k, :],
                                   start=k == 0, stop=k == TOP1 // P - 1)
                mm.then_inc(top2_done, 1)
            for k in range(TOP2 // P):
                pe.wait_ge(h2_ready, k + 1)
                mm = pe.matmul(acc2[0][0:1, :], wt3_sb[:, k:k + 1], h2[:, k, :], start=k == 0, stop=k == TOP2 // P - 1)
            mm.then_inc(top3_done, 1)


def shift_rows():
    p, i, k = np.meshgrid(np.arange(P), np.arange(SHIFTS), np.arange(SHIFTS), indexing="ij")
    return ((p + i) % HID) * FIELDS + (p + SHIFTS * k) % FIELDS


def pair_fields():
    p, m, k = np.meshgrid(np.arange(P), np.arange(PAIR_SHIFTS), np.arange(1, 5), indexing="ij")
    f = (p + m + PAIR_SHIFTS * (p >= FIELDS)) % FIELDS
    g = (p + SHIFTS * k) % FIELDS
    return f.reshape(P, 16), g.reshape(P, 16)


def kernel(**inputs):
    import concourse.bacc as bacc
    from concourse.bass_utils import run_bass_kernel_spmd as run

    a = {k: np.asarray(v) for k, v in inputs.items()}
    table_list = [a[f"tbl_{f}"] for f in range(FIELDS)]
    sizes = np.array([t.shape[0] for t in table_list])
    first_row = np.concatenate([[0], np.cumsum(sizes)[:-1]])
    info = np.tile(np.stack([sizes, sizes - 1, first_row], axis=1), (2, 1)).astype(np.float32)

    ids = a["ids"].reshape(CHUNKS, 2, HALF_B, FIELDS).transpose(1, 3, 0, 2).reshape(P, CHUNKS * HALF_B)

    w0 = a["L0_rec_W0"]
    f, g = pair_fields()
    w0a = np.zeros((P, 17, HID), np.float32)
    w0b = np.zeros((P, 17, HID), np.float32)
    w0a[:, 0:16] = w0[:, f * FIELDS + g].transpose(1, 2, 0)
    once = (f - g) % FIELDS == FIELDS // 2
    w0b[:, 0:16] = w0[:, g * FIELDS + f].transpose(1, 2, 0)
    w0b[:, 0:16][once] = 0
    w0a[0:FIELDS, 16] = w0[:, np.arange(FIELDS) * (FIELDS + 1)].T
    w1 = a["L0_rec_W1"][:, shift_rows().reshape(P, -1)].transpose(1, 2, 0)
    w2 = a["L0_rec_W2"].reshape(HID, HID, FIELDS).transpose(1, 2, 0)

    arrays = {
        "ids": ids, "field_info": info, "tables": np.concatenate(table_list, axis=0), "dense": a["dense_ctx"].T,
        "w0a": w0a, "w0b": w0b.reshape(P, 17 * HID), "w1": w1, "w2": w2,
        "bias": np.stack([a["L0_rec_b0"], a["L0_rec_b1"], a["L0_rec_b2"]], axis=1),
        "wt1": a["W_top1"][0:3 * HID].reshape(3, P, TOP1).transpose(1, 0, 2), "wt1d": a["W_top1"][3 * HID:],
        "bt1": a["b_top1"].reshape(TOP1 // P, P).T, "wt2": a["W_top2"].reshape(TOP1 // P, P, TOP2).transpose(1, 0, 2),
        "bt2": a["b_top2"].reshape(TOP2 // P, P).T, "wt3": a["W_top3"].reshape(TOP2 // P, P).T,
        "ident": np.eye(P, dtype=np.float32),
        "mask": (np.arange(P)[:, None] // EMBED == np.arange(GROUP_B)[None, :]).astype(np.float32),
    }
    arrays = {k: np.ascontiguousarray(v) for k, v in arrays.items()}
    nc = bacc.Bacc("TRN2", target_bir_lowering=False, num_devices=1)
    aps = {k: nc.dram_tensor(f"in_{k}", v.shape, mybir.dt.from_np(v.dtype), kind="ExternalInput").ap()
           for k, v in arrays.items()}
    out = nc.dram_tensor("out_y", (BATCH, 1), F32, kind="ExternalOutput").ap()
    build(nc, out=out, **aps)
    got = run(nc, [{f"in_{k}": v for k, v in arrays.items()}], core_ids=[0])
    return got.results[0]["out_y"]
```

```python
from contextlib import ExitStack

import numpy as np

import concourse.bass as bass
from concourse import mybir

F32 = mybir.dt.float32
F32R = mybir.dt.float32r
I32 = mybir.dt.int32
ALU = mybir.AluOpType
ACT = mybir.ActivationFunctionType
AX = mybir.AxisListType

P = 128
BATCH, FIELDS, EMBED, HID, DENSE = 512, 64, 16, 128, 16
COLS = 512
CHUNK_B = COLS // EMBED
CHUNKS = BATCH // CHUNK_B
HALF_B = CHUNK_B // 2
SHIFTS = 8
PAIR_SHIFTS = 4
QUAD = 4
GROUP_B = P // EMBED
BLOCKS = CHUNK_B // GROUP_B
X0_ROWS = 3 * FIELDS
X1_ROWS = HID + SHIFTS
L2_GROUPS = SHIFTS * SHIFTS // QUAD // QUAD
GROUPS = 1 + L2_GROUPS
ALL_GROUPS = CHUNKS * GROUPS
SPLIT_UNITS = 3
L1_SPLIT = SPLIT_UNITS * QUAD
L2_SPLIT = L2_GROUPS * SPLIT_UNITS * QUAD
SPLIT_TILES = L1_SPLIT + L2_SPLIT
L1_PLAIN, L2_PLAIN = QUAD, L2_GROUPS * QUAD
Z_SLOT = {0: 0, 1: 1, 3: 2}
SPLIT_SLOT = {1: 0, 3: 1, 2: 2}
L1_PAIR = {1: 0, 0: 1, 2: 2, 3: 3}
COPIES = PAIR_SHIFTS + SHIFTS
LAND_SLOTS = 3
F_BLOCK = 16
TOP1, TOP2 = 512, 256


class Chunk:

    def __init__(self, n, r):
        self.n, self.r = n, r
        self.par = r % 2

    def plus(self, k):
        return Chunk(self.n, self.r + k)

    def is_(self, number):
        return isinstance(self.n, int) and 2 * self.n + self.r == number

    def count(self, per_chunk, more=0):
        if isinstance(self.n, int):
            return per_chunk * (2 * self.n + self.r) + more
        return self.n * (2 * per_chunk) + (per_chunk * self.r + more)

    def turn(self, per_turn, more=0):
        if isinstance(self.n, int):
            return per_turn * (self.n + self.r // 2) + more
        return self.n * per_turn + (per_turn * (self.r // 2) + more)


class Group:

    def __init__(self, chunk, j, k=None):
        self.chunk, self.j, self.k = chunk, j, k
        self.is_first = chunk.is_(0) and j == -1

    def count(self, per_group, more=0):
        return self.chunk.count(GROUPS * per_group, per_group * (1 + self.j) + more)

    def copies(self, more=0):
        return self.chunk.count(COPIES, PAIR_SHIFTS + self.k + more)

    def land_slot(self, n):
        return (PAIR_SHIFTS + self.k + n) % LAND_SLOTS

    def landed(self, n):
        return self.chunk.count(16 * COPIES // LAND_SLOTS, 16 * ((PAIR_SHIFTS + self.k + n) // LAND_SLOTS + 1))


def layer1_group(c):
    if c.is_(0):
        return Group(c, -1, -PAIR_SHIFTS)
    if c.is_(1):
        return Group(c.plus(-1), 0, 0)
    return Group(c.plus(-1), 2, 4)


def layer2_group(c, i):
    if c.is_(0):
        return Group(c, i + 1, PAIR_SHIFTS + 2 * i)
    if i < 2 or c.is_(CHUNKS - 1):
        return Group(c, i, 2 * i)
    return Group(c, i + 1, PAIR_SHIFTS + 2 * i)


def build(nc, ids, field_info, tables, dense, w0a, w0b, w0a_split, w0b_split, w1, w1_split, w2, bias, wt1, wt1d, bt1, wt2, bt2, wt3, ident, mask, out):
    x0_scratch = nc.dram_tensor("x0_scratch", (CHUNKS, X0_ROWS, COLS), F32, kind="Internal").ap()
    x1_scratch = nc.dram_tensor("x1_scratch", (CHUNKS, X1_ROWS, COLS), F32, kind="Internal").ap()
    gram_scratch = nc.dram_tensor("gram_scratch", (HID, 2 * CHUNKS, FIELDS, HALF_B), F32, kind="Internal").ap()

    with ExitStack() as ctx:
        def sb(name, shape, dt=F32):
            return ctx.enter_context(nc.sbuf_tensor(name, shape, dt))

        def ps(name, shape):
            return ctx.enter_context(nc.psum_tensor(name, shape, F32))

        def sem(name):
            return ctx.enter_context(nc.semaphore(name))

        def sb_twice(name, other, shape):
            with nc.sbuf_tensor(other, shape, F32) as whole:
                pass
            return ctx.enter_context(nc.sbuf_tensor(name, shape, F32R)), whole

        rows = sb("rows", [P, CHUNKS * HALF_B], I32)
        rows_chunk = sb("rows_chunk", [P, 2, HALF_B], I32)
        info_sb = sb("info_sb", [P, 3])
        bias_sb = sb("bias_sb", [P, 3])
        bias3_sb = sb("bias3_sb", [P, 1])
        w0_sb = sb("w0_sb", [P, L1_PLAIN + 1, HID])
        w1_sb = sb("w1_sb", [P, L2_PLAIN, HID])
        w_hi = sb("w_hi", [P, SPLIT_TILES, HID], F32R)
        w_lo, w_whole = sb_twice("w_lo", "w_whole", [P, SPLIT_TILES, HID])
        wt3_sb = sb("wt3_sb", [P, TOP2 // P])
        bt1_sb = sb("bt1_sb", [P, TOP1 // P])
        bt2_sb = sb("bt2_sb", [P, TOP2 // P])
        ident_sb = sb("ident_sb", [P, P])
        mask_sb = sb("mask_sb", [P, GROUP_B])
        emb = sb("emb", [P, 2, HALF_B * EMBED])
        x0_shift = sb("x0_shift", [P, 2, SHIFTS, COLS])
        land = sb("land", [P, LAND_SLOTS, COLS])
        z = sb("z", [P, len(Z_SLOT), QUAD, COLS])
        z_hi, z_hi_whole = sb_twice("z_hi", "z_hi_whole", [P, len(SPLIT_SLOT), QUAD, COLS])
        z_lo, z_lo_whole = sb_twice("z_lo", "z_lo_whole", [P, len(SPLIT_SLOT), QUAD, COLS])
        z_sq = sb("z_sq", [FIELDS, COLS])
        x1 = sb("x1", [P, COLS])
        x2 = sb("x2", [P, COLS])
        x2t = sb("x2t", [P, COLS])
        blocks = sb("blocks", [P, 2, GROUP_B, FIELDS])
        gram = sb("gram", [P, FIELDS, HALF_B])
        sums = sb("sums", [P, 3, BATCH])

        work = gram[:, :, :].rearrange("p f b -> p (f b)")
        ids_sb, ids_tmp, rows_f = (work[:, k * CHUNKS * HALF_B:(k + 1) * CHUNKS * HALF_B] for k in range(3))
        ids_sb = ids_sb.bitcast(I32)
        z_flat = z[:, :, :, :].rearrange("p a q n -> p (a q n)")
        w0b_split_stage = z_flat[:, 0:L1_SPLIT * HID].rearrange("p (t o) -> p t o", o=HID)
        w0b_stage = z_flat[:, L1_SPLIT * HID:(L1_SPLIT + L1_PLAIN + 1) * HID]
        wt1_sb, wt1d_sb = x0_shift[:, 0, 0:3, :], x0_shift[0:DENSE, 0, 3, :]
        dense_sb = emb[0:DENSE, :, :].rearrange("p a n -> p (a n)")
        w2_first = x0_shift[:, 0, 4:8, :].rearrange("p k (t o) -> p (k t) o", o=HID)
        w2_parts = [w2_first] + [w_whole[:, k * F_BLOCK:(k + 1) * F_BLOCK, :] for k in range(3)]
        gram_buffers = [b.rearrange("p c (f b) -> p c f b", f=F_BLOCK) for b in (
            z[:, 0:2].rearrange("p a q (h n) -> p (a q h) n", h=2),
            z_hi_whole[:, 0:2].rearrange("p a q (h n) -> p (a q h) n", h=2),
            z_lo_whole[:, 0:2].rearrange("p a q (h n) -> p (a q h) n", h=2),
            x0_shift[:, 1].rearrange("p k (h n) -> p (k h) n", h=2))]
        wt2_sb = z_hi_whole[:, 2, 0:2, :].rearrange("p a (h n) -> p (a h) n", h=2)
        h1, h2, y_sb = z[:, 2], z_lo_whole[:, 2], z_sq[0:1, :]
        F_BLOCKS = FIELDS // F_BLOCK
        GRAM_LOADS = 2 * F_BLOCKS
        GRAM_BUFFERS = len(gram_buffers)

        acc1 = ps("acc1", [P, COLS])
        acc2 = ps("acc2", [P, COLS])
        operand = [ps("operand_even", [P, COLS]), ps("operand_odd", [P, COLS])]
        z_ps = ps("z_ps", [P, 2, COLS])
        turn_gram_ps = ps("turn_gram_ps", [P, COLS])
        x0t_ps = ps("x0t_ps", [P, 2 * BLOCKS, FIELDS])

        ids_in, const_in, w0_in, w1_in, w1_split_in, top_in = (sem(s) for s in ("ids_in", "const_in", "w0_in", "w1_in", "w1_split_in", "top_in"))
        wt2_in = sem("wt2_in")
        w2_in = [sem(f"w2_in_{k}") for k in range(F_BLOCKS)]
        w_rounded, w_split = sem("w_rounded"), sem("w_split")
        rows_step, rows_ready, rows_copied, gather_begun = (sem(s) for s in ("rows_step", "rows_ready", "rows_copied", "gather_begun"))
        w0_summed = sem("w0_summed")
        gathered = [sem("gathered_even"), sem("gathered_odd")]
        x0_stored = [sem("x0_stored_even"), sem("x0_stored_odd")]
        x0_loaded = [sem("x0_loaded_even"), sem("x0_loaded_odd")]
        x0_rest_loaded = [sem("x0_rest_loaded_even"), sem("x0_rest_loaded_odd")]
        x1_stored, gram_stored = sem("x1_stored"), sem("gram_stored")
        landed = [sem(f"landed_{s}") for s in range(LAND_SLOTS)]
        copied, squared = sem("copied"), sem("squared")
        formed = sem("formed")
        halves_formed = sem("halves_formed")
        rounded = sem("rounded")
        halves_rounded = sem("halves_rounded")
        subtracted = sem("subtracted")
        halves_split = sem("halves_split")
        used = sem("used")
        half_used = sem("half_used")
        x2_turned, x0_turned, gram_done = (sem(s) for s in ("x2_turned", "x0_turned", "gram_done"))
        x1_ready, x2_ready, x2t_ready, gram_staged = (sem(s) for s in ("x1_ready", "x2_ready", "x2t_ready", "gram_staged"))
        sum1_ready, sum2_ready, sum3_ready, block_ready = (sem(s) for s in ("sum1_ready", "sum2_ready", "sum3_ready", "block_ready"))
        bias3_ready = sem("bias3_ready")
        gram_loaded = [sem(f"gram_loaded_{s}") for s in range(GRAM_BUFFERS)]
        gram_used, sp_passed = sem("gram_used"), sem("sp_passed")
        top1_done, top2_done, top3_done = sem("top1_done"), sem("top2_done"), sem("top3_done")
        h1_ready, h2_ready, y_ready, y_stored = sem("h1_ready"), sem("h2_ready"), sem("y_ready"), sem("y_stored")

        block = ctx.enter_context(nc.Block())

        @block.sync
        def _(sp):
            def at(*offsets):
                return [x if isinstance(x, int) else sp.compute_val(x) for x in offsets]

            def wait_all(*waits):
                for s, value in [(s, at(value)[0]) for s, value in waits]:
                    sp.wait_ge(s, value)
                sp.sem_inc(sp_passed, 1)

            sp.dma_start(ids_sb, ids).then_inc(ids_in, 16)
            sp.dma_start(info_sb[:, :], field_info).then_inc(ids_in, 16)
            sp.dma_start(w_whole[:, 0:L1_SPLIT, :], w0a_split).then_inc(w0_in, 16)
            sp.dma_start(w0b_split_stage, w0b_split).then_inc(w0_in, 16)
            sp.dma_start(w0_sb[:, :, :], w0a).then_inc(w0_in, 16)
            sp.dma_start(w0b_stage, w0b).then_inc(w0_in, 16)
            sp.dma_start(w_whole[:, L1_SPLIT:, :], w1_split).then_inc(w1_split_in, 16)
            for t, s in ((bias_sb, bias), (ident_sb, ident), (mask_sb, mask)):
                sp.dma_start(t[:, :], s).then_inc(const_in, 16)
            sp.dma_start(w1_sb[:, :, :], w1).then_inc(w1_in, 16)

            def store_x0(c):
                offsets = at(*(c.count(X0_ROWS * COLS, s * (COLS // 2)) for s in range(2)))
                wait_all((gathered[c.par], c.turn(16 * HALF_B, 16 * HALF_B)))
                for s in range(2):
                    src = emb[s * FIELDS:(s + 1) * FIELDS, c.par, :].rearrange("p (r n) -> p r n", r=1)
                    dst = bass.AP(x0_scratch.tensor, offsets[s],
                                  [[COLS, FIELDS], [FIELDS * COLS, 3], [1, COLS // 2]])
                    sp.dma_start(dst, src.to_broadcast([FIELDS, 3, COLS // 2])).then_inc(x0_stored[c.par], 16)

            def load_copies(c, first, end, loaded, *waits):
                offset, = at(c.count(X0_ROWS * COLS, first * SHIFTS * COLS))
                wait_all(*waits)
                sp.dma_start(x0_shift[:, c.par, first:end], bass.AP(
                    x0_scratch.tensor, offset,
                    [[COLS, P], [SHIFTS * COLS, end - first], [1, COLS]])).then_inc(loaded[c.par], 16)

            def load_x0(c):
                waits = [(x0_stored[c.par], c.turn(32, 32))]
                if not (c.is_(0) or c.is_(1)):
                    waits.append((halves_formed, Group(c.plus(-2), 4).count(2, 2)))
                load_copies(c, 1, 5, x0_loaded, *waits)
                load_copies(c, 5, SHIFTS, x0_rest_loaded)

            def load_x0_base(c):
                if c.is_(0) or c.is_(1):
                    load_copies(c, 0, 1, x0_rest_loaded)
                else:
                    load_copies(c, 0, 1, x0_rest_loaded,
                                (x0_turned, c.count(1, -1)))

            def load_pair(c, m):
                g = layer1_group(c)
                offset, = at(c.count(X0_ROWS * COLS, m * COLS))
                slot = g.land_slot(m)
                waits = []
                if not (c.is_(0) and m < LAND_SLOTS):
                    waits.append((copied, g.copies(m - LAND_SLOTS + 1)))
                if m == LAND_SLOTS:
                    waits.append((squared, c.count(1, 1)))
                wait_all(*waits)
                sp.dma_start(land[:, slot, :], bass.AP(
                    x0_scratch.tensor, offset,
                    [[(FIELDS + PAIR_SHIFTS) * COLS, 2], [COLS, FIELDS], [1, COLS]])).then_inc(landed[slot], 16)

            def store_x1(c):
                offsets = at(c.count(X1_ROWS * COLS), c.count(X1_ROWS * COLS, HID * COLS))
                wait_all((x1_ready, c.count(1, 1)))
                for offset, n in zip(offsets, (HID, SHIFTS)):
                    sp.dma_start(bass.AP(x1_scratch.tensor, offset, [[COLS, n], [1, COLS]]),
                                 x1[0:n, :]).then_inc(x1_stored, 16)

            def load_shift(c, i):
                g, n = layer2_group(c, i // 2), i % 2
                offset, = at(c.count(X1_ROWS * COLS, i * COLS))
                waits = [(copied, g.copies(n - LAND_SLOTS + 1))]
                if i == 0:
                    waits.append((x1_stored, c.count(32, 32)))
                wait_all(*waits)
                sp.dma_start(land[:, g.land_slot(n), :], bass.AP(
                    x1_scratch.tensor, offset, [[COLS, P], [1, COLS]])).then_inc(landed[g.land_slot(n)], 16)

            def store_gram(c, half):
                offset, = at(c.count(2 * FIELDS * HALF_B, half * FIELDS * HALF_B))
                wait_all((gram_staged, c.count(BLOCKS, 2 * half + 2)))
                sp.dma_start(bass.AP(gram_scratch.tensor, offset,
                                     [[2 * CHUNKS * FIELDS * HALF_B, HID], [1, FIELDS * HALF_B]]),
                             gram[:, :, :].rearrange("p f b -> p (f b)")).then_inc(gram_stored, 16)

            def round_(c, near_end=False):
                prev, nxt = c.plus(-1), c.plus(1)
                load_x0(nxt)
                load_pair(nxt, 0)
                load_pair(nxt, 1)
                load_x0_base(nxt)
                if not c.is_(1):
                    store_gram(c.plus(-2), 1)
                load_pair(nxt, 2)
                load_pair(nxt, 3)
                for i in range(4, SHIFTS):
                    load_shift(c, i)
                store_gram(prev, 0)
                store_x1(nxt)
                for i in range(LAND_SLOTS):
                    load_shift(nxt, i)
                load_shift(nxt, 3)
                if not near_end:
                    store_x0(c.plus(2))

            c0, c1 = Chunk(0, 0), Chunk(0, 1)
            store_x0(c0)
            sp.wait_ge(x0_stored[0], 32)
            load_pair(c0, 0)
            load_x0(c0)
            load_pair(c0, 1)
            load_pair(c0, 2)
            load_x0_base(c0)
            load_pair(c0, 3)
            store_x0(c1)
            load_x0(c1)
            for m in range(PAIR_SHIFTS):
                load_pair(c1, m)
            store_x1(c0)
            load_x0_base(c1)
            for i in range(5):
                load_shift(c0, i)
            store_x1(c1)
            for t, s in ((bt1_sb[:, :], bt1), (bt2_sb[:, :], bt2), (wt3_sb[:, :], wt3)):
                sp.dma_start(t, s).then_inc(top_in, 16)
            for i in range(5, SHIFTS):
                load_shift(c0, i)
            for i in range(4):
                load_shift(c1, i)
            store_x0(c0.plus(2))
            round_(c1)
            with sp.Fori(0, (CHUNKS - 4) // 2) as n:
                round_(Chunk(n, 2))
                round_(Chunk(n, 3))
            end = Chunk(0, CHUNKS - 1)
            round_(end.plus(-1), near_end=True)
            for par in range(2):
                sp.wait_ge(x0_stored[par], 16 * CHUNKS)
            sp.dma_start(dense_sb, dense).then_inc(top_in, 16)
            sp.wait_ge(halves_formed, Group(end.plus(-1), 4).count(2, 2))
            sp.wait_ge(x0_turned, CHUNKS - 1)
            sp.dma_start(wt1_sb, wt1).then_inc(top_in, 16)
            sp.dma_start(wt1d_sb, wt1d).then_inc(top_in, 16)
            sp.dma_start(w2_parts[0], w2[:, 0:F_BLOCK, :]).then_inc(w2_in[0], 16)
            for i in range(4, SHIFTS - 1):
                load_shift(end, i)
            store_gram(end.plus(-2), 1)
            load_shift(end, SHIFTS - 1)
            store_gram(end.plus(-1), 0)

            def load_gram(k):
                half, fb = k // F_BLOCKS, k % F_BLOCKS
                sp.dma_start(gram_buffers[k % GRAM_BUFFERS].rearrange("p c f b -> p c (f b)"), bass.AP(
                    gram_scratch.tensor, (half * CHUNKS * FIELDS + fb * F_BLOCK) * HALF_B,
                    [[2 * CHUNKS * FIELDS * HALF_B, HID], [FIELDS * HALF_B, CHUNKS], [1, F_BLOCK * HALF_B]],
                )).then_inc(gram_loaded[k % GRAM_BUFFERS], 16)

            sp.wait_ge(gram_stored, 2 * 16 * (CHUNKS - 2))
            sp.wait_ge(used, QUAD * ALL_GROUPS)
            load_gram(0)
            sp.dma_start(w2_parts[1], w2[:, F_BLOCK:2 * F_BLOCK, :]).then_inc(w2_in[1], 16)
            store_gram(end.plus(-1), 1)
            load_gram(1)
            store_gram(end, 0)
            sp.wait_ge(x0_turned, CHUNKS)
            for k in range(2, F_BLOCKS):
                sp.dma_start(w2_parts[k], w2[:, k * F_BLOCK:(k + 1) * F_BLOCK, :]).then_inc(w2_in[k], 16)
                load_gram(k)
            store_gram(end, 1)
            sp.dma_start(wt2_sb, wt2).then_inc(wt2_in, 16)
            sp.wait_ge(gram_stored, 2 * 16 * CHUNKS)
            for k in range(GRAM_BUFFERS, GRAM_LOADS):
                sp.wait_ge(gram_used, k - GRAM_BUFFERS + 1)
                load_gram(k)
            sp.wait_ge(y_ready, 1)
            sp.dma_start(out.rearrange("b o -> o b"), y_sb).then_inc(y_stored, 16)
            sp.wait_ge(y_stored, 16)
            sp.wait_ge(x1_stored, 32 * CHUNKS)

        @block.gpsimd
        def _(pool):
            def take_rows(c, first=False):
                if not first:
                    pool.wait_ge(x0_stored[c.par], c.turn(32))
                pool.tensor_copy(rows_chunk[:, c.par, :], rows[:, bass.ds(c.count(HALF_B), HALF_B)]).then_inc(rows_copied, 1)
                pool.wait_ge(rows_copied, c.count(1, 1))
                pool.sem_inc(gather_begun, 1)

            def gather(c, js):
                for j in js:
                    pool.indirect_dma_start(
                        out=emb[:, c.par, j * EMBED:(j + 1) * EMBED], out_offset=None, in_=tables,
                        in_offset=bass.IndirectOffsetOnAxis(ap=rows_chunk[:, c.par, j:j + 1], axis=0),
                    ).then_inc(gathered[c.par], 16)

            def low_part(g, pos):
                slot = SPLIT_SLOT[pos]
                pool.wait_ge(rounded, g.count(2, (pos + 1) // 2))
                pool.tensor_tensor(z_lo[:, slot], z[:, Z_SLOT[pos]], z_hi[:, slot].bitcast(F32),
                                   ALU.subtract).then_inc(subtracted, 1)

            def round_(c, look_up=True, groups=GROUPS):
                if look_up:
                    take_rows(c.plus(2))
                done = 0
                for j in range(groups):
                    for pos in (1, 3):
                        low_part(Group(c, j), pos)
                        if look_up:
                            upto = -(-HALF_B * (2 * j + pos // 2 + 1) // (2 * groups))
                            gather(c.plus(2), range(done, upto))
                            done = upto

            pool.wait_ge(rows_ready, 1)
            for c in (Chunk(0, 0), Chunk(0, 1)):
                take_rows(c, first=True)
                gather(c, range(HALF_B))
            with pool.Fori(0, (CHUNKS - 2) // 2) as n:
                round_(Chunk(n, 0))
                round_(Chunk(n, 1))
            round_(Chunk(0, CHUNKS - 2), look_up=False)
            round_(Chunk(0, CHUNKS - 1), look_up=False, groups=L2_GROUPS)

        @block.vector
        def _(dve):
            dve.wait_ge(ids_in, 32)
            dve.tensor_scalar(ids_tmp, ids_sb, 0.0, info_sb[:, 0:1], ALU.is_lt, ALU.mult).then_inc(rows_step, 1)
            dve.wait_ge(rows_step, 1)
            dve.tensor_tensor(rows_f, ids_tmp, ids_sb, ALU.add).then_inc(rows_step, 1)
            dve.wait_ge(rows_step, 2)
            dve.tensor_scalar(ids_tmp, rows_f, 0.0, info_sb[:, 1:2], ALU.max, ALU.min).then_inc(rows_step, 1)
            dve.wait_ge(rows_step, 3)
            dve.tensor_scalar(rows[:, :], ids_tmp, info_sb[:, 2:3], None, ALU.add).then_inc(rows_ready, 1)
            dve.wait_ge(w0_in, 64)
            w0_flat = w0_sb[:, :, :].rearrange("p t o -> p (t o)")
            dve.tensor_tensor(w_whole[:, 0:L1_SPLIT, :], w_whole[:, 0:L1_SPLIT, :], w0b_split_stage, ALU.add).then_inc(w0_summed, 1)
            dve.tensor_tensor(w0_flat, w0_flat, w0b_stage, ALU.add).then_inc(w0_summed, 1)

            def split_weights(step, tiles):
                dve.wait_ge(w_rounded, step)
                dve.tensor_tensor(w_lo[:, tiles, :], w_whole[:, tiles, :], w_hi[:, tiles, :].bitcast(F32),
                                  ALU.subtract).then_inc(w_split, 1)

            split_weights(1, slice(0, L1_SPLIT))
            split_weights(2, slice(L1_SPLIT, SPLIT_TILES))
            dve.wait_ge(const_in, 48)
            dve.tensor_scalar(bias3_sb[:, :], bias_sb[:, 2:3], float(EMBED), None, ALU.mult).then_inc(bias3_ready, 1)
            dve.wait_ge(w0_summed, 2)

            def times(bank, tiles, x0_tiles):
                return operand[bank][:, :].rearrange("p (q n) -> p q n", q=1).to_broadcast([P, tiles, COLS]), x0_tiles

            def form(g, pos, bank, x0_tiles):
                if not g.is_first:
                    if pos == 0:
                        dve.wait_ge(used, g.count(4, -3))
                    else:
                        dve.wait_ge(subtracted, g.count(2, -2 + (pos + 1) // 2))
                dve.tensor_tensor(z[:, Z_SLOT[pos]], *times(bank, QUAD, x0_tiles), ALU.mult).then_inc(formed, 1)

            def form_half(g, half, bank, x0_tiles):
                if not g.is_first or half:
                    dve.wait_ge(halves_split, g.count(2, half))
                dve.tensor_tensor(z_ps[:, :, :], *times(bank, 2, x0_tiles), ALU.mult).then_inc(halves_formed, 1)

            def split_half(g, half):
                dve.wait_ge(halves_rounded, g.count(2, half + 1))
                tiles = slice(2 * half, 2 * half + 2)
                dve.tensor_tensor(z_lo[:, SPLIT_SLOT[2], tiles], z_ps[:, :, :],
                                  z_hi[:, SPLIT_SLOT[2], tiles].bitcast(F32), ALU.subtract).then_inc(halves_split, 1)

            def layer1(c, pos, half=None):
                g, pair = layer1_group(c), L1_PAIR[pos]
                if half != 1:
                    dve.wait_ge(copied, g.copies(pair + 1))
                if pair == 0:
                    dve.wait_ge(x0_loaded[c.par], c.turn(16, 16))
                if half is None:
                    form(g, pos, pair % 2, x0_shift[:, c.par, 1:5])
                else:
                    form_half(g, half, pair % 2, x0_shift[:, c.par, 1 + 2 * half:3 + 2 * half])

            def layer2(c, i, pos, half=None):
                g = layer2_group(c, i)
                if pos in (1, 2) and half != 1:
                    dve.wait_ge(copied, g.copies(pos // 2 + 1))
                if i == 0 and pos == 1:
                    dve.wait_ge(x0_rest_loaded[c.par], c.turn(32, 32))
                tile = QUAD * (pos % 2)
                if half is None:
                    form(g, pos, pos // 2, x0_shift[:, c.par, tile:tile + QUAD])
                else:
                    form_half(g, half, pos // 2, x0_shift[:, c.par, tile + 2 * half:tile + 2 * half + 2])

            def form_block(c, b):
                if b == 0:
                    dve.wait_ge(x0_turned, c.count(1, 1))
                if not (c.is_(0) and b < 2):
                    dve.wait_ge(gram_done, c.count(BLOCKS, b - 1))
                dve.tensor_tensor(
                    blocks[:, b % 2], x0t_ps[:, b:b + 1, :].to_broadcast([P, GROUP_B, FIELDS]),
                    mask_sb[:, :].rearrange("p (b f) -> p b f", f=1).to_broadcast([P, GROUP_B, FIELDS]),
                    ALU.mult).then_inc(block_ready, 1)

            def sum1(c):
                dve.wait_ge(x1_ready, c.count(1, 1))
                dve.tensor_reduce(sums[:, 0, bass.ds(c.count(CHUNK_B), CHUNK_B)],
                                  x1[:, :].rearrange("p (b d) -> p b d", d=EMBED), AX.X, ALU.add).then_inc(sum1_ready, 1)

            def sum2(c):
                dve.wait_ge(x2_ready, c.count(1, 1))
                dve.tensor_reduce(sums[:, 1, bass.ds(c.count(CHUNK_B), CHUNK_B)],
                                  x2[:, :].rearrange("p (b d) -> p b d", d=EMBED), AX.X, ALU.add).then_inc(sum2_ready, 1)

            def layer2_middle(c, i):
                layer2(c, i, 2, half=0)
                layer2(c, i, 3)
                split_half(layer2_group(c, i), 0)
                layer2(c, i, 2, half=1)

            def layer1_middle(c):
                layer1(c, 2, half=0)
                layer1(c, 3)
                split_half(layer1_group(c), 0)
                layer1(c, 2, half=1)

            def round_(c):
                prev, nxt = c.plus(-1), c.plus(1)
                layer2_middle(c, 0)
                layer2(c, 1, 1)
                split_half(layer2_group(c, 0), 1)
                sum1(c)
                layer2(c, 1, 0)
                layer2_middle(c, 1)
                form_block(prev, 0)
                layer1(nxt, 1)
                split_half(layer2_group(c, 1), 1)
                sum2(prev)
                layer1(nxt, 0)
                form_block(prev, 1)
                layer1_middle(nxt)
                form_block(prev, 2)
                layer2(c, 2, 1)
                split_half(layer1_group(nxt), 1)
                layer2(c, 2, 0)
                layer2_middle(c, 2)
                layer2(c, 3, 1)
                split_half(layer2_group(c, 2), 1)
                layer2(c, 3, 0)
                layer2_middle(c, 3)
                form_block(prev, 3)
                layer2(nxt, 0, 1)
                split_half(layer2_group(c, 3), 1)
                layer2(nxt, 0, 0)

            c0, c1 = Chunk(0, 0), Chunk(0, 1)
            g0 = layer1_group(c0)
            def low_part(pos):
                dve.wait_ge(rounded, (pos + 1) // 2)
                slot = SPLIT_SLOT[pos]
                dve.tensor_tensor(z_lo[:, slot], z[:, Z_SLOT[pos]], z_hi[:, slot].bitcast(F32), ALU.subtract).then_inc(subtracted, 1)

            layer1(c0, 1)
            layer1(c0, 0)
            low_part(1)
            layer1_middle(c0)
            low_part(3)
            split_half(g0, 1)
            layer1(c1, 1)
            layer1(c1, 0)
            layer1_middle(c1)
            split_half(layer1_group(c1), 1)
            sum1(c0)
            layer2(c0, 0, 1)
            layer2(c0, 0, 0)
            for i in range(L2_GROUPS):
                layer2_middle(c0, i)
                after = (c0, i + 1) if i < L2_GROUPS - 1 else (c1, 0)
                layer2(*after, 1)
                split_half(layer2_group(c0, i), 1)
                layer2(*after, 0)
            round_(c1)
            with dve.Fori(0, (CHUNKS - 4) // 2) as n:
                round_(Chunk(n, 2))
                round_(Chunk(n, 3))
            end = Chunk(0, CHUNKS - 1)
            round_(end.plus(-1))
            prev = end.plus(-1)
            layer2_middle(end, 0)
            layer2(end, 1, 1)
            split_half(layer2_group(end, 0), 1)
            sum1(end)
            layer2(end, 1, 0)
            layer2_middle(end, 1)
            form_block(prev, 0)
            layer2(end, 2, 1)
            split_half(layer2_group(end, 1), 1)
            sum2(prev)
            layer2(end, 2, 0)
            form_block(prev, 1)
            layer2_middle(end, 2)
            form_block(prev, 2)
            layer2(end, 3, 1)
            split_half(layer2_group(end, 2), 1)
            layer2(end, 3, 0)
            form_block(prev, 3)
            layer2_middle(end, 3)
            split_half(layer2_group(end, 3), 1)
            for b in range(BLOCKS):
                form_block(end, b)
            sum2(end)

        @block.scalar
        def _(act):
            def to_bank(g, n, bank, released=None):
                slot = g.land_slot(n)
                act.wait_ge(landed[slot], g.landed(n))
                if released is not None:
                    act.wait_ge(*released)
                act.activation(operand[bank][:, :], land[:, slot, :], ACT.Copy).then_inc(copied, 1)

            def released_by_layer2(g, bank):
                return (formed, g.count(3, 2)) if bank == 0 else (halves_formed, g.count(2, 2))

            def released_by_layer1(g, bank):
                return (halves_formed, g.count(2, 2)) if bank == 0 else (formed, g.count(3, 3))

            def round_unit(g, pos):
                act.wait_ge(formed, g.count(3, pos))
                if not g.is_first:
                    act.wait_ge(used, g.count(4, pos - 3))
                act.activation(z_hi[:, SPLIT_SLOT[pos]], z[:, Z_SLOT[pos]], ACT.Copy).then_inc(rounded, 1)

            def round_half(g, half):
                act.wait_ge(halves_formed, g.count(2, half + 1))
                if not g.is_first:
                    if half == 0:
                        act.wait_ge(half_used, g.count(1))
                    else:
                        act.wait_ge(used, g.count(4, -1))
                act.activation(z_hi[:, SPLIT_SLOT[2], 2 * half:2 * half + 2], z_ps[:, :, :], ACT.Copy).then_inc(halves_rounded, 1)

            def square(c):
                if not c.is_(0):
                    act.wait_ge(used, layer1_group(c.plus(-1)).count(4, 1))
                act.activation(z_sq[:, :], land[0:FIELDS, layer1_group(c).land_slot(0), :], ACT.Square).then_inc(squared, 1)

            def take_x1(c):
                act.wait_ge(used, layer1_group(c).count(4, 4))
                if not c.is_(0):
                    act.wait_ge(x1_stored, c.count(32))
                    act.wait_ge(sum1_ready, c.count(1))
                act.activation(x1[:, :], acc1[:, :], ACT.Identity, bias=bias_sb[:, 0:1]).then_inc(x1_ready, 1)

            def take_x2(c):
                act.wait_ge(used, layer2_group(c, 3).count(4, 4))
                if not c.is_(0):
                    act.wait_ge(sum2_ready, c.count(1))
                    act.wait_ge(x2_turned, c.count(1))
                act.activation(x2[:, :], acc2[:, :], ACT.Identity, bias=bias_sb[:, 1:2]).then_inc(x2_ready, 1)

            def take_x2t(c):
                act.wait_ge(x2_turned, c.count(1, 1))
                if not c.is_(0):
                    act.wait_ge(gram_done, c.count(BLOCKS))
                act.activation(x2t[:, :], turn_gram_ps[:, :], ACT.Copy).then_inc(x2t_ready, 1)

            def take_gram(c, b):
                act.wait_ge(gram_done, c.count(BLOCKS, b + 1))
                if b % 2 == 0 and not (c.is_(0) and b == 0):
                    act.wait_ge(gram_stored, c.count(32, 16 * (b // 2)))
                act.activation(gram[:, :, b % 2 * GROUP_B:(b % 2 + 1) * GROUP_B].rearrange("p f b -> p b f"),
                               turn_gram_ps[:, :].rearrange("p (b f) -> p b f", f=FIELDS), ACT.Copy).then_inc(gram_staged, 1)

            def round_(c):
                prev, nxt = c.plus(-1), c.plus(1)
                a, b, m, d, e, f = (layer2_group(c, 0), layer2_group(c, 1), layer1_group(nxt),
                                    layer2_group(c, 2), layer2_group(c, 3), layer2_group(nxt, 0))
                to_bank(b, 0, 0, released_by_layer2(a, 0))
                round_half(a, 0)
                take_x2(prev)
                round_unit(a, 3)
                if not c.is_(1):
                    take_gram(c.plus(-2), 3)
                round_half(a, 1)
                to_bank(b, 1, 1, released_by_layer2(a, 1))
                round_unit(b, 1)

                to_bank(m, 0, 0, released_by_layer2(b, 0))
                round_half(b, 0)
                take_x2t(prev)
                round_unit(b, 3)
                square(nxt)
                round_half(b, 1)
                to_bank(m, 1, 1, released_by_layer2(b, 1))
                to_bank(m, 2, 0, (formed, m.count(3, 1)))
                round_unit(m, 1)

                to_bank(m, 3, 1, (formed, m.count(3, 2)))
                round_half(m, 0)
                take_gram(prev, 0)
                round_unit(m, 3)
                to_bank(d, 0, 0, released_by_layer1(m, 0))
                round_half(m, 1)
                to_bank(d, 1, 1, released_by_layer1(m, 1))
                round_unit(d, 1)

                to_bank(e, 0, 0, released_by_layer2(d, 0))
                round_half(d, 0)
                round_unit(d, 3)
                take_gram(prev, 1)
                round_half(d, 1)
                to_bank(e, 1, 1, released_by_layer2(d, 1))
                take_x1(nxt)
                round_unit(e, 1)

                to_bank(f, 0, 0, released_by_layer2(e, 0))
                round_half(e, 0)
                round_unit(e, 3)
                take_gram(prev, 2)
                round_half(e, 1)
                to_bank(f, 1, 1, released_by_layer2(e, 1))
                round_unit(f, 1)

            c0, c1 = Chunk(0, 0), Chunk(0, 1)
            g0, g1 = layer1_group(c0), layer1_group(c1)
            act.wait_ge(w0_summed, 1)
            act.activation(w_hi[:, 0:L1_SPLIT, :], w_whole[:, 0:L1_SPLIT, :], ACT.Copy).then_inc(w_rounded, 1)
            act.wait_ge(w1_split_in, 16)
            act.activation(w_hi[:, L1_SPLIT:, :], w_whole[:, L1_SPLIT:, :], ACT.Copy).then_inc(w_rounded, 1)
            to_bank(g0, 0, 0)
            to_bank(g0, 1, 1)
            square(c0)
            to_bank(g0, 2, 0, (formed, 1))
            round_unit(g0, 1)
            to_bank(g0, 3, 1, (formed, 2))
            round_half(g0, 0)
            round_unit(g0, 3)
            round_half(g0, 1)
            to_bank(g1, 0, 0, released_by_layer1(g0, 0))
            to_bank(g1, 1, 1, released_by_layer1(g0, 1))
            square(c1)
            act.wait_ge(const_in, 48)
            take_x1(c0)
            to_bank(g1, 2, 0, (formed, g1.count(3, 1)))
            round_unit(g1, 1)
            to_bank(g1, 3, 1, (formed, g1.count(3, 2)))
            round_half(g1, 0)
            round_unit(g1, 3)
            round_half(g1, 1)
            first = layer2_group(c0, 0)
            to_bank(first, 0, 0, released_by_layer1(g1, 0))
            to_bank(first, 1, 1, released_by_layer1(g1, 1))
            round_unit(first, 1)
            for i in range(L2_GROUPS):
                g = layer2_group(c0, i)
                after = layer2_group(c0, i + 1) if i < L2_GROUPS - 1 else layer2_group(c1, 0)
                to_bank(after, 0, 0, released_by_layer2(g, 0))
                round_half(g, 0)
                round_unit(g, 3)
                if i == 0:
                    take_x1(c1)
                round_half(g, 1)
                to_bank(after, 1, 1, released_by_layer2(g, 1))
                round_unit(after, 1)
            round_(c1)
            with act.Fori(0, (CHUNKS - 4) // 2) as n:
                round_(Chunk(n, 2))
                round_(Chunk(n, 3))
            end = Chunk(0, CHUNKS - 1)
            prev = end.plus(-1)
            round_(prev)
            for i in range(L2_GROUPS):
                g = layer2_group(end, i)
                after = layer2_group(end, i + 1) if i < L2_GROUPS - 1 else None
                if after:
                    to_bank(after, 0, 0, released_by_layer2(g, 0))
                round_half(g, 0)
                if i == 0:
                    take_x2(prev)
                if i == 1:
                    take_x2t(prev)
                if i == 2:
                    take_gram(prev, 0)
                round_unit(g, 3)
                if i == 0:
                    take_gram(end.plus(-2), 3)
                if i == 3:
                    take_gram(prev, 1)
                round_half(g, 1)
                if after:
                    to_bank(after, 1, 1, released_by_layer2(g, 1))
                    round_unit(after, 1)
            take_gram(prev, 2)
            take_x2(end)
            take_gram(prev, 3)
            take_x2t(end)
            for b in range(BLOCKS):
                take_gram(end, b)
            act.wait_ge(gram_used, GRAM_LOADS)
            act.wait_ge(bias3_ready, 1)
            act.activation(sums[:, 2, :], z_ps[:, 1, :], ACT.Identity, bias=bias3_sb[:, 0:1]).then_inc(sum3_ready, 1)
            act.wait_ge(top_in, 6 * 16)
            for m, bank in enumerate((acc1[:, :], operand[0][:, :], operand[1][:, :], z_ps[:, 0, :])):
                act.wait_ge(top1_done, m + 1)
                act.activation(h1[:, m, :], bank, ACT.Relu, bias=bt1_sb[:, m:m + 1]).then_inc(h1_ready, 1)
            for m, bank in enumerate((turn_gram_ps[:, :], x0t_ps[:, :, :].rearrange("p b f -> p (b f)"))):
                act.wait_ge(top2_done, m + 1)
                act.activation(h2[:, m, :], bank, ACT.Relu, bias=bt2_sb[:, m:m + 1]).then_inc(h2_ready, 1)
            act.wait_ge(top3_done, 1)
            act.activation(y_sb, acc2[0:1, :], ACT.Copy).then_inc(y_ready, 1)

        @block.tensor
        def _(pe):
            def float_unit(g, acc, weights, tile0, start=False):
                pe.wait_ge(formed, g.count(3, 2))
                for q in range(QUAD):
                    mm = pe.matmul(acc[:, :], weights[:, tile0 + q, :], z[:, Z_SLOT[0], q, :], start=start and q == 0, stop=False)
                mm.then_inc(used, 1)

            def split_tile(acc, tile, slot, q, stop):
                for n, (w, zz) in enumerate(((w_hi, z_hi), (w_hi, z_lo), (w_lo, z_hi))):
                    mm = pe.matmul(acc[:, :], w[:, tile, :], zz[:, slot, q, :], start=False, stop=stop and n == 2)
                return mm

            def split_unit(g, pos, acc, tile0, stop=False):
                pe.wait_ge(subtracted, g.count(2, (pos + 1) // 2))
                for q in range(QUAD):
                    mm = split_tile(acc, tile0 + q, SPLIT_SLOT[pos], q, stop and q == QUAD - 1)
                mm.then_inc(used, 1)

            def halves_unit(g, acc, tile0):
                for half, done in enumerate((half_used, used)):
                    pe.wait_ge(halves_split, g.count(2, half + 1))
                    for q in (2 * half, 2 * half + 1):
                        mm = split_tile(acc, tile0 + q, SPLIT_SLOT[2], q, False)
                    mm.then_inc(done, 1)

            def layer1(c):
                g = layer1_group(c)
                pe.wait_ge(squared, c.count(1, 1))
                if not c.is_(0):
                    pe.wait_ge(x1_ready, c.count(1))
                pe.matmul(acc1[:, :], w0_sb[0:FIELDS, L1_PLAIN, :], z_sq[:, :], start=True, stop=False)
                float_unit(g, acc1, w0_sb, 0)
                split_unit(g, 1, acc1, 0)
                halves_unit(g, acc1, QUAD)
                split_unit(g, 3, acc1, 2 * QUAD, stop=True)

            def layer2(c, i, positions):
                g = layer2_group(c, i)
                for pos in positions:
                    tile0 = L1_SPLIT + (SPLIT_UNITS * i + pos - 1) * QUAD
                    if pos == 0:
                        if i == 0 and not c.is_(0):
                            pe.wait_ge(x2_ready, c.count(1))
                        float_unit(g, acc2, w1_sb, QUAD * i, start=i == 0)
                    elif pos == 2:
                        halves_unit(g, acc2, tile0)
                    else:
                        if i == L2_GROUPS - 1 and pos == 3 and not c.is_(0):
                            pe.wait_ge(block_ready, c.count(BLOCKS))
                        split_unit(g, pos, acc2, tile0, stop=i == L2_GROUPS - 1 and pos == 3)

            def turn_x0(c):
                for b in range(BLOCKS):
                    t = pe.transpose(x0t_ps[:, b, :], x0_shift[0:FIELDS, c.par, 0, b * P:(b + 1) * P],
                                     ident_sb[0:FIELDS, 0:FIELDS])
                t.then_inc(x0_turned, 1)

            def turn_x2(c):
                if not c.is_(0):
                    pe.wait_ge(gram_staged, c.count(BLOCKS))
                pe.wait_ge(x2_ready, c.count(1, 1))
                for b in range(BLOCKS):
                    t = pe.transpose(turn_gram_ps[:, b * P:(b + 1) * P], x2[:, b * P:(b + 1) * P], ident_sb[:, :])
                t.then_inc(x2_turned, 1)

            def gram_of(c, b):
                if b == 0:
                    pe.wait_ge(x2t_ready, c.count(1, 1))
                else:
                    pe.wait_ge(gram_staged, c.count(BLOCKS, b))
                pe.wait_ge(block_ready, c.count(BLOCKS, b + 1))
                pe.matmul(turn_gram_ps[:, :], x2t[:, b * P:(b + 1) * P],
                          blocks[:, b % 2].rearrange("p b f -> p (b f)"), start=True, stop=True).then_inc(gram_done, 1)

            def round_(c, last=False):
                prev = c.plus(-1)
                layer2(c, 0, (0, 1))
                turn_x2(prev)
                layer2(c, 0, (2, 3))
                layer2(c, 1, (0,))
                gram_of(prev, 0)
                layer2(c, 1, (1, 2, 3))
                if not last:
                    layer1(c.plus(1))
                layer2(c, 2, (0,))
                gram_of(prev, 1)
                layer2(c, 2, (1, 2, 3))
                layer2(c, 3, (0,))
                gram_of(prev, 2)
                layer2(c, 3, (1, 2, 3))
                turn_x0(c)
                gram_of(prev, 3)

            c0 = Chunk(0, 0)
            pe.wait_ge(w0_summed, 2)
            pe.wait_ge(w_split, 1)
            layer1(c0)
            layer1(c0.plus(1))
            pe.wait_ge(w1_in, 16)
            pe.wait_ge(w_split, 2)
            pe.wait_ge(const_in, 48)
            for i in range(L2_GROUPS):
                layer2(c0, i, range(QUAD))
            turn_x0(c0)
            round_(c0.plus(1))
            with pe.Fori(0, (CHUNKS - 4) // 2) as n:
                round_(Chunk(n, 2))
                round_(Chunk(n, 3))
            end = Chunk(0, CHUNKS - 1)
            round_(end.plus(-1))
            round_(end, last=True)

            top_banks = (acc1[:, :], operand[0][:, :], operand[1][:, :], z_ps[:, 0, :])

            def top1_begin(m):
                pe.matmul(top_banks[m], wt1d_sb[:, m * P:(m + 1) * P], dense_sb, start=True, stop=False)
                pe.matmul(top_banks[m], wt1_sb[:, 0, m * P:(m + 1) * P], sums[:, 0, :], start=False, stop=False)

            pe.wait_ge(top_in, 6 * 16)
            pe.wait_ge(sum1_ready, CHUNKS)
            pe.wait_ge(halves_split, 2 * ALL_GROUPS)
            top1_begin(0)
            turn_x2(end)
            top1_begin(1)
            gram_of(end, 0)
            top1_begin(2)
            gram_of(end, 1)
            top1_begin(3)

            half_b = BATCH // 2
            for k in range(GRAM_LOADS):
                half, fb = k // F_BLOCKS, k % F_BLOCKS
                pe.wait_ge(gram_loaded[k % GRAM_BUFFERS], 16 * (k // GRAM_BUFFERS + 1))
                pe.wait_ge(w2_in[fb], 16)
                for f in range(F_BLOCK):
                    mm = pe.matmul(z_ps[:, 1, half * half_b:(half + 1) * half_b], w2_parts[fb][:, f, :],
                                   gram_buffers[k % GRAM_BUFFERS][:, :, f, :], start=fb == 0 and f == 0,
                                   stop=fb == F_BLOCKS - 1 and f == F_BLOCK - 1)
                mm.then_inc(gram_used, 1)
                if k < 2:
                    gram_of(end, 2 + k)
                if k == 1:
                    pe.wait_ge(sum2_ready, CHUNKS)
                    for m in range(TOP1 // P):
                        pe.matmul(top_banks[m], wt1_sb[:, 1, m * P:(m + 1) * P], sums[:, 1, :], start=False, stop=False)

            pe.wait_ge(sum3_ready, 1)
            for m in range(TOP1 // P):
                pe.matmul(top_banks[m], wt1_sb[:, 2, m * P:(m + 1) * P], sums[:, 2, :],
                          start=False, stop=True).then_inc(top1_done, 1)
            pe.wait_ge(wt2_in, 16)
            for m, bank in enumerate((turn_gram_ps[:, :], x0t_ps[:, :, :].rearrange("p b f -> p (b f)"))):
                for k in range(TOP1 // P):
                    if m == 0:
                        pe.wait_ge(h1_ready, k + 1)
                    mm = pe.matmul(bank, wt2_sb[:, k, m * P:(m + 1) * P], h1[:, k, :],
                                   start=k == 0, stop=k == TOP1 // P - 1)
                mm.then_inc(top2_done, 1)
            for k in range(TOP2 // P):
                pe.wait_ge(h2_ready, k + 1)
                mm = pe.matmul(acc2[0:1, :], wt3_sb[:, k:k + 1], h2[:, k, :], start=k == 0, stop=k == TOP2 // P - 1)
            mm.then_inc(top3_done, 1)


def shift_rows():
    p, i, k = np.meshgrid(np.arange(P), np.arange(SHIFTS), np.arange(SHIFTS), indexing="ij")
    return ((p + i) % HID) * FIELDS + (p + SHIFTS * k) % FIELDS


def pair_fields():
    p, m, k = np.meshgrid(np.arange(P), np.arange(PAIR_SHIFTS), np.arange(1, 5), indexing="ij")
    f = (p + m + PAIR_SHIFTS * (p >= FIELDS)) % FIELDS
    g = (p + SHIFTS * k) % FIELDS
    return f.reshape(P, 16), g.reshape(P, 16)


def kernel(**inputs):
    import concourse.bacc as bacc
    from concourse.bass_utils import run_bass_kernel_spmd as run

    a = {k: np.asarray(v) for k, v in inputs.items()}
    table_list = [a[f"tbl_{f}"] for f in range(FIELDS)]
    sizes = np.array([t.shape[0] for t in table_list])
    first_row = np.concatenate([[0], np.cumsum(sizes)[:-1]])
    info = np.tile(np.stack([sizes, sizes - 1, first_row], axis=1), (2, 1)).astype(np.float32)

    ids = a["ids"].reshape(CHUNKS, 2, HALF_B, FIELDS).transpose(1, 3, 0, 2).reshape(P, CHUNKS * HALF_B)

    w0 = a["L0_rec_W0"]
    f, g = pair_fields()
    once = (f - g) % FIELDS == FIELDS // 2
    pairs = w0[:, f * FIELDS + g].transpose(1, 2, 0).reshape(P, 1, QUAD, QUAD * HID)
    pairs_turned = w0[:, g * FIELDS + f].transpose(1, 2, 0)
    pairs_turned[once] = 0
    pairs_turned = pairs_turned.reshape(P, 1, QUAD, QUAD * HID)
    squares = np.zeros((P, HID), np.float32)
    squares[0:FIELDS] = w0[:, np.arange(FIELDS) * (FIELDS + 1)].T
    w1 = a["L0_rec_W1"][:, shift_rows().reshape(P, -1)].transpose(1, 2, 0).reshape(P, L2_GROUPS, QUAD, QUAD * HID)
    w2 = a["L0_rec_W2"].reshape(HID, HID, FIELDS).transpose(1, 2, 0)

    arrays = {
        "ids": ids, "field_info": info, "tables": np.concatenate(table_list, axis=0), "dense": a["dense_ctx"].T,
        "w0a": np.concatenate([pairs[:, :, 1].reshape(P, -1), squares], axis=1).reshape(P, L1_PLAIN + 1, HID),
        "w0b": np.concatenate([pairs_turned[:, :, 1].reshape(P, -1), np.zeros_like(squares)], axis=1),
        "w0a_split": pairs[:, :, [0, 2, 3]].reshape(P, L1_SPLIT, HID), "w0b_split": pairs_turned[:, :, [0, 2, 3]].reshape(P, L1_SPLIT, HID),
        "w1": w1[:, :, 0].reshape(P, L2_PLAIN, HID), "w1_split": w1[:, :, 1:].reshape(P, L2_SPLIT, HID), "w2": w2,
        "bias": np.stack([a["L0_rec_b0"], a["L0_rec_b1"], a["L0_rec_b2"]], axis=1),
        "wt1": a["W_top1"][0:3 * HID].reshape(3, P, TOP1).transpose(1, 0, 2), "wt1d": a["W_top1"][3 * HID:],
        "bt1": a["b_top1"].reshape(TOP1 // P, P).T, "wt2": a["W_top2"].reshape(TOP1 // P, P, TOP2).transpose(1, 0, 2),
        "bt2": a["b_top2"].reshape(TOP2 // P, P).T, "wt3": a["W_top3"].reshape(TOP2 // P, P).T,
        "ident": np.eye(P, dtype=np.float32),
        "mask": (np.arange(P)[:, None] // EMBED == np.arange(GROUP_B)[None, :]).astype(np.float32),
    }
    arrays = {k: np.ascontiguousarray(v) for k, v in arrays.items()}
    nc = bacc.Bacc("TRN2", target_bir_lowering=False, num_devices=1)
    aps = {k: nc.dram_tensor(f"in_{k}", v.shape, mybir.dt.from_np(v.dtype), kind="ExternalInput").ap()
           for k, v in arrays.items()}
    out = nc.dram_tensor("out_y", (BATCH, 1), F32, kind="ExternalOutput").ap()
    build(nc, out=out, **aps)
    got = run(nc, [{f"in_{k}": v for k, v in arrays.items()}], core_ids=[0])
    return got.results[0]["out_y"]
```

```python
from contextlib import ExitStack

import numpy as np

import concourse.bass as bass
from concourse import mybir

F32 = mybir.dt.float32
F32R = mybir.dt.float32r
I32 = mybir.dt.int32
ALU = mybir.AluOpType
ACT = mybir.ActivationFunctionType
AX = mybir.AxisListType

P = 128
BATCH, FIELDS, EMBED, HID, DENSE = 512, 64, 16, 128, 16
COLS = 512
CHUNK_B = COLS // EMBED
CHUNKS = BATCH // CHUNK_B
HALF_B = CHUNK_B // 2
SHIFTS = 8
PAIR_SHIFTS = 4
QUAD = 4
GROUP_B = P // EMBED
BLOCKS = CHUNK_B // GROUP_B
X0_ROWS = 3 * FIELDS
X1_ROWS = HID + SHIFTS
L2_GROUPS = SHIFTS * SHIFTS // QUAD // QUAD
GROUPS = 1 + L2_GROUPS
ALL_GROUPS = CHUNKS * GROUPS
SPLIT_UNITS = 3
L1_SPLIT = SPLIT_UNITS * QUAD
L2_SPLIT = L2_GROUPS * SPLIT_UNITS * QUAD
SPLIT_TILES = L1_SPLIT + L2_SPLIT
L1_PLAIN, L2_PLAIN = QUAD, L2_GROUPS * QUAD
Z_SLOT = {0: 0, 1: 1, 3: 2}
SPLIT_SLOT = {1: 0, 3: 1, 2: 2}
L1_PAIR = {1: 0, 0: 1, 2: 2, 3: 3}
COPIES = PAIR_SHIFTS + SHIFTS
LAND_SLOTS = 3
W2_PART = 16
F_BLOCK = 8
HALF_BLOCKS = FIELDS // F_BLOCK
GRAM_BLOCKS = 2 * HALF_BLOCKS
PLAIN_BLOCKS = W2_PART // F_BLOCK
TOP1, TOP2 = 512, 256


def is_plain(k):
    return k % HALF_BLOCKS < PLAIN_BLOCKS


def splits_before(k):
    return sum(not is_plain(n) for n in range(k))


class Chunk:

    def __init__(self, n, r):
        self.n, self.r = n, r
        self.par = r % 2

    def plus(self, k):
        return Chunk(self.n, self.r + k)

    def is_(self, number):
        return isinstance(self.n, int) and 2 * self.n + self.r == number

    def count(self, per_chunk, more=0):
        if isinstance(self.n, int):
            return per_chunk * (2 * self.n + self.r) + more
        return self.n * (2 * per_chunk) + (per_chunk * self.r + more)

    def turn(self, per_turn, more=0):
        if isinstance(self.n, int):
            return per_turn * (self.n + self.r // 2) + more
        return self.n * per_turn + (per_turn * (self.r // 2) + more)


class Group:

    def __init__(self, chunk, j, k=None):
        self.chunk, self.j, self.k = chunk, j, k
        self.is_first = chunk.is_(0) and j == -1

    def count(self, per_group, more=0):
        return self.chunk.count(GROUPS * per_group, per_group * (1 + self.j) + more)

    def copies(self, more=0):
        return self.chunk.count(COPIES, PAIR_SHIFTS + self.k + more)

    def land_slot(self, n):
        return (PAIR_SHIFTS + self.k + n) % LAND_SLOTS

    def landed(self, n):
        return self.chunk.count(16 * COPIES // LAND_SLOTS, 16 * ((PAIR_SHIFTS + self.k + n) // LAND_SLOTS + 1))


def layer1_group(c):
    if c.is_(0):
        return Group(c, -1, -PAIR_SHIFTS)
    if c.is_(1):
        return Group(c.plus(-1), 0, 0)
    return Group(c.plus(-1), 2, 4)


def layer2_group(c, i):
    if c.is_(0):
        return Group(c, i + 1, PAIR_SHIFTS + 2 * i)
    if i < 2 or c.is_(CHUNKS - 1):
        return Group(c, i, 2 * i)
    return Group(c, i + 1, PAIR_SHIFTS + 2 * i)


def build(nc, ids, field_info, tables, dense, w0a, w0b, w0a_split, w0b_split, w1, w1_split, w2, bias, wt1, wt1d, bt1, wt2, bt2, wt3, ident, mask, out):
    x0_scratch = nc.dram_tensor("x0_scratch", (CHUNKS, X0_ROWS, COLS), F32, kind="Internal").ap()
    x1_scratch = nc.dram_tensor("x1_scratch", (CHUNKS, X1_ROWS, COLS), F32, kind="Internal").ap()
    gram_scratch = nc.dram_tensor("gram_scratch", (HID, 2 * CHUNKS, FIELDS, HALF_B), F32, kind="Internal").ap()

    with ExitStack() as ctx:
        def sb(name, shape, dt=F32):
            return ctx.enter_context(nc.sbuf_tensor(name, shape, dt))

        def ps(name, shape):
            return ctx.enter_context(nc.psum_tensor(name, shape, F32))

        def sem(name):
            return ctx.enter_context(nc.semaphore(name))

        def sb_twice(name, other, shape):
            with nc.sbuf_tensor(other, shape, F32) as whole:
                pass
            return ctx.enter_context(nc.sbuf_tensor(name, shape, F32R)), whole

        rows = sb("rows", [P, CHUNKS * HALF_B], I32)
        rows_chunk = sb("rows_chunk", [P, 2, HALF_B], I32)
        info_sb = sb("info_sb", [P, 3])
        bias_sb = sb("bias_sb", [P, 3])
        bias3_sb = sb("bias3_sb", [P, 1])
        w0_sb = sb("w0_sb", [P, L1_PLAIN + 1, HID])
        w1_sb = sb("w1_sb", [P, L2_PLAIN, HID])
        w_hi = sb("w_hi", [P, SPLIT_TILES, HID], F32R)
        w_lo, w_whole = sb_twice("w_lo", "w_whole", [P, SPLIT_TILES, HID])
        wt3_sb = sb("wt3_sb", [P, TOP2 // P])
        bt1_sb = sb("bt1_sb", [P, TOP1 // P])
        bt2_sb = sb("bt2_sb", [P, TOP2 // P])
        ident_sb = sb("ident_sb", [P, P])
        mask_sb = sb("mask_sb", [P, GROUP_B])
        emb = sb("emb", [P, 2, HALF_B * EMBED])
        x0_shift = sb("x0_shift", [P, 2, SHIFTS, COLS])
        land = sb("land", [P, LAND_SLOTS, COLS])
        z = sb("z", [P, len(Z_SLOT), QUAD, COLS])
        z_hi = sb("z_hi", [P, len(SPLIT_SLOT), QUAD, COLS], F32R)
        z_lo, z_lo_whole = sb_twice("z_lo", "z_lo_whole", [P, len(SPLIT_SLOT), QUAD, COLS])
        z_sq = sb("z_sq", [FIELDS, COLS])
        x1 = sb("x1", [P, COLS])
        x2 = sb("x2", [P, COLS])
        x2t = sb("x2t", [P, COLS])
        blocks = sb("blocks", [P, 2, GROUP_B, FIELDS])
        gram = sb("gram", [P, FIELDS, HALF_B])
        sums = sb("sums", [P, 3, BATCH])

        work = gram[:, :, :].rearrange("p f b -> p (f b)")
        ids_sb, ids_tmp, rows_f = (work[:, k * CHUNKS * HALF_B:(k + 1) * CHUNKS * HALF_B] for k in range(3))
        ids_sb = ids_sb.bitcast(I32)
        z_flat = z[:, :, :, :].rearrange("p a q n -> p (a q n)")
        w0b_split_stage = z_flat[:, 0:L1_SPLIT * HID].rearrange("p (t o) -> p t o", o=HID)
        w0b_stage = z_flat[:, L1_SPLIT * HID:(L1_SPLIT + L1_PLAIN + 1) * HID]
        wt1_sb, wt1d_sb = x0_shift[:, 0, 0:3, :], x0_shift[0:DENSE, 0, 3, :]
        dense_sb = emb[0:DENSE, :, :].rearrange("p a n -> p (a n)")
        w2_first = x0_shift[:, 0, 4:8, :].rearrange("p k (t o) -> p (k t) o", o=HID)
        w2_parts = [w2_first] + [w_whole[:, k * W2_PART:(k + 1) * W2_PART, :] for k in range(3)]

        def gram_view(b):
            return b.rearrange("p q (h n) -> p (q h) n", h=CHUNKS // QUAD).rearrange("p c (f b) -> p c f b", f=F_BLOCK)

        gram_buffers = [gram_view(b) for b in (z[:, 0], z[:, 1], z[:, 2], x0_shift[:, 1, 0:QUAD], x0_shift[:, 1, QUAD:])]
        GRAM_BUFFERS = len(gram_buffers)
        gram_hi, gram_lo = ([gram_view(b[:, slot]) for slot in range(len(SPLIT_SLOT))] for b in (z_hi, z_lo))
        GRAM_SLOTS = len(gram_hi)
        wt2_sb = land[:, 0:2, :].rearrange("p a (h n) -> p (a h) n", h=2)
        h1, h2, y_sb = z[:, 2], z_lo_whole[:, 2], z_sq[0:1, :]

        acc1 = ps("acc1", [P, COLS])
        acc2 = ps("acc2", [P, COLS])
        operand = [ps("operand_even", [P, COLS]), ps("operand_odd", [P, COLS])]
        z_ps = ps("z_ps", [P, 2, COLS])
        turn_gram_ps = ps("turn_gram_ps", [P, COLS])
        x0t_ps = ps("x0t_ps", [P, 2 * BLOCKS, FIELDS])

        ids_in, const_in, w0_in, w1_in, w1_split_in, top_in = (sem(s) for s in ("ids_in", "const_in", "w0_in", "w1_in", "w1_split_in", "top_in"))
        wt2_in = sem("wt2_in")
        w2_in = [sem(f"w2_in_{k}") for k in range(FIELDS // W2_PART)]
        w2_rounded, w2_split = sem("w2_rounded"), sem("w2_split")
        gram_rounded, gram_split = sem("gram_rounded"), sem("gram_split")
        w_rounded, w_split = sem("w_rounded"), sem("w_split")
        rows_step, rows_ready, rows_free, rows_copied, gather_begun = (
            sem(s) for s in ("rows_step", "rows_ready", "rows_free", "rows_copied", "gather_begun"))
        w0_summed = sem("w0_summed")
        gathered = [sem("gathered_even"), sem("gathered_odd")]
        x0_stored = [sem("x0_stored_even"), sem("x0_stored_odd")]
        x0_loaded = [sem("x0_loaded_even"), sem("x0_loaded_odd")]
        x0_rest_loaded = [sem("x0_rest_loaded_even"), sem("x0_rest_loaded_odd")]
        x1_stored, gram_stored = sem("x1_stored"), sem("gram_stored")
        landed = [sem(f"landed_{s}") for s in range(LAND_SLOTS)]
        copied, squared = sem("copied"), sem("squared")
        formed = sem("formed")
        halves_formed = sem("halves_formed")
        rounded = sem("rounded")
        halves_rounded = sem("halves_rounded")
        subtracted = sem("subtracted")
        halves_split = sem("halves_split")
        used = sem("used")
        half_used = sem("half_used")
        x2_turned, x0_turned, gram_done = (sem(s) for s in ("x2_turned", "x0_turned", "gram_done"))
        x1_ready, x2_ready, x2t_ready, gram_staged = (sem(s) for s in ("x1_ready", "x2_ready", "x2t_ready", "gram_staged"))
        sum1_ready, sum2_ready, sum3_ready, block_ready = (sem(s) for s in ("sum1_ready", "sum2_ready", "sum3_ready", "block_ready"))
        bias3_ready = sem("bias3_ready")
        gram_loaded = [sem(f"gram_loaded_{s}") for s in range(GRAM_BUFFERS)]
        gram_used, sp_passed = sem("gram_used"), sem("sp_passed")
        top1_done, top2_done, top3_done = sem("top1_done"), sem("top2_done"), sem("top3_done")
        h1_ready, h2_ready, y_ready, y_stored = sem("h1_ready"), sem("h2_ready"), sem("y_ready"), sem("y_stored")

        block = ctx.enter_context(nc.Block())

        @block.sync
        def _(sp):
            def at(*offsets):
                return [x if isinstance(x, int) else sp.compute_val(x) for x in offsets]

            def wait_all(*waits):
                for s, value in [(s, at(value)[0]) for s, value in waits]:
                    sp.wait_ge(s, value)
                sp.sem_inc(sp_passed, 1)

            sp.dma_start(ids_sb, ids).then_inc(ids_in, 16)
            sp.dma_start(info_sb[:, :], field_info).then_inc(ids_in, 16)
            sp.dma_start(w_whole[:, 0:L1_SPLIT, :], w0a_split).then_inc(w0_in, 16)
            sp.dma_start(w0b_split_stage, w0b_split).then_inc(w0_in, 16)
            sp.dma_start(w0_sb[:, :, :], w0a).then_inc(w0_in, 16)
            sp.dma_start(w0b_stage, w0b).then_inc(w0_in, 16)
            sp.dma_start(w_whole[:, L1_SPLIT:, :], w1_split).then_inc(w1_split_in, 16)
            for t, s in ((bias_sb, bias), (ident_sb, ident), (mask_sb, mask)):
                sp.dma_start(t[:, :], s).then_inc(const_in, 16)
            sp.dma_start(w1_sb[:, :, :], w1).then_inc(w1_in, 16)

            def store_x0(c):
                offsets = at(*(c.count(X0_ROWS * COLS, s * (COLS // 2)) for s in range(2)))
                wait_all((gathered[c.par], c.turn(16 * HALF_B, 16 * HALF_B)))
                for s in range(2):
                    src = emb[s * FIELDS:(s + 1) * FIELDS, c.par, :].rearrange("p (r n) -> p r n", r=1)
                    dst = bass.AP(x0_scratch.tensor, offsets[s],
                                  [[COLS, FIELDS], [FIELDS * COLS, 3], [1, COLS // 2]])
                    sp.dma_start(dst, src.to_broadcast([FIELDS, 3, COLS // 2])).then_inc(x0_stored[c.par], 16)

            def load_copies(c, first, end, loaded, *waits):
                offset, = at(c.count(X0_ROWS * COLS, first * SHIFTS * COLS))
                wait_all(*waits)
                sp.dma_start(x0_shift[:, c.par, first:end], bass.AP(
                    x0_scratch.tensor, offset,
                    [[COLS, P], [SHIFTS * COLS, end - first], [1, COLS]])).then_inc(loaded[c.par], 16)

            def load_x0(c):
                waits = [(x0_stored[c.par], c.turn(32, 32))]
                if not (c.is_(0) or c.is_(1)):
                    waits.append((halves_formed, Group(c.plus(-2), 4).count(2, 2)))
                load_copies(c, 1, 5, x0_loaded, *waits)

            def load_x0_rest(c):
                load_copies(c, 5, SHIFTS, x0_rest_loaded)

            def load_x0_base(c):
                if c.is_(0) or c.is_(1):
                    load_copies(c, 0, 1, x0_rest_loaded)
                else:
                    load_copies(c, 0, 1, x0_rest_loaded,
                                (x0_turned, c.count(1, -1)))

            def load_pair(c, m):
                g = layer1_group(c)
                offset, = at(c.count(X0_ROWS * COLS, m * COLS))
                slot = g.land_slot(m)
                waits = []
                if not (c.is_(0) and m < LAND_SLOTS):
                    waits.append((copied, g.copies(m - LAND_SLOTS + 1)))
                if m == LAND_SLOTS:
                    waits.append((squared, c.count(1, 1)))
                wait_all(*waits)
                sp.dma_start(land[:, slot, :], bass.AP(
                    x0_scratch.tensor, offset,
                    [[(FIELDS + PAIR_SHIFTS) * COLS, 2], [COLS, FIELDS], [1, COLS]])).then_inc(landed[slot], 16)

            def store_x1(c):
                offsets = at(c.count(X1_ROWS * COLS), c.count(X1_ROWS * COLS, HID * COLS))
                wait_all((x1_ready, c.count(1, 1)))
                for offset, n in zip(offsets, (HID, SHIFTS)):
                    sp.dma_start(bass.AP(x1_scratch.tensor, offset, [[COLS, n], [1, COLS]]),
                                 x1[0:n, :]).then_inc(x1_stored, 16)

            def load_shift(c, i):
                g, n = layer2_group(c, i // 2), i % 2
                offset, = at(c.count(X1_ROWS * COLS, i * COLS))
                waits = [(copied, g.copies(n - LAND_SLOTS + 1))]
                if i == 0:
                    waits.append((x1_stored, c.count(32, 32)))
                wait_all(*waits)
                sp.dma_start(land[:, g.land_slot(n), :], bass.AP(
                    x1_scratch.tensor, offset, [[COLS, P], [1, COLS]])).then_inc(landed[g.land_slot(n)], 16)

            def store_gram(c, half):
                offset, = at(c.count(2 * FIELDS * HALF_B, half * FIELDS * HALF_B))
                wait_all((gram_staged, c.count(BLOCKS, 2 * half + 2)))
                sp.dma_start(bass.AP(gram_scratch.tensor, offset,
                                     [[2 * CHUNKS * FIELDS * HALF_B, HID], [1, FIELDS * HALF_B]]),
                             gram[:, :, :].rearrange("p f b -> p (f b)")).then_inc(gram_stored, 16)

            def round_(c, near_end=False):
                prev, nxt = c.plus(-1), c.plus(1)
                load_x0(nxt)
                load_x0_rest(nxt)
                load_pair(nxt, 0)
                load_pair(nxt, 1)
                load_x0_base(nxt)
                if not c.is_(1):
                    store_gram(c.plus(-2), 1)
                load_pair(nxt, 2)
                load_pair(nxt, 3)
                for i in range(4, SHIFTS):
                    load_shift(c, i)
                store_gram(prev, 0)
                store_x1(nxt)
                for i in range(LAND_SLOTS):
                    load_shift(nxt, i)
                load_shift(nxt, 3)
                if not near_end:
                    store_x0(c.plus(2))

            c0, c1 = Chunk(0, 0), Chunk(0, 1)
            store_x0(c0)
            sp.wait_ge(x0_stored[0], 32)
            load_pair(c0, 0)
            load_x0(c0)
            load_pair(c0, 1)
            load_pair(c0, 2)
            load_x0_rest(c0)
            load_x0_base(c0)
            load_pair(c0, 3)
            store_x0(c1)
            load_x0(c1)
            for m in range(PAIR_SHIFTS):
                load_pair(c1, m)
            load_x0_rest(c1)
            store_x1(c0)
            load_x0_base(c1)
            for i in range(5):
                load_shift(c0, i)
            store_x1(c1)
            for t, s in ((bt1_sb[:, :], bt1), (bt2_sb[:, :], bt2), (wt3_sb[:, :], wt3)):
                sp.dma_start(t, s).then_inc(top_in, 16)
            for i in range(5, SHIFTS):
                load_shift(c0, i)
            for i in range(4):
                load_shift(c1, i)
            store_x0(c0.plus(2))
            round_(c1)
            with sp.Fori(0, (CHUNKS - 4) // 2) as n:
                round_(Chunk(n, 2))
                round_(Chunk(n, 3))
            end = Chunk(0, CHUNKS - 1)
            round_(end.plus(-1), near_end=True)
            for par in range(2):
                sp.wait_ge(x0_stored[par], 16 * CHUNKS)
            sp.dma_start(dense_sb, dense).then_inc(top_in, 16)
            sp.wait_ge(halves_formed, Group(end.plus(-1), 4).count(2, 2))
            sp.wait_ge(x0_turned, CHUNKS - 1)
            sp.dma_start(wt1_sb, wt1).then_inc(top_in, 16)
            sp.dma_start(wt1d_sb, wt1d).then_inc(top_in, 16)
            sp.dma_start(w2_parts[0], w2[:, 0:W2_PART, :]).then_inc(w2_in[0], 16)

            def load_gram(k):
                half, fb = k // HALF_BLOCKS, k % HALF_BLOCKS
                sp.dma_start(gram_buffers[k % GRAM_BUFFERS].rearrange("p c f b -> p c (f b)"), bass.AP(
                    gram_scratch.tensor, (half * CHUNKS * FIELDS + fb * F_BLOCK) * HALF_B,
                    [[2 * CHUNKS * FIELDS * HALF_B, HID], [FIELDS * HALF_B, CHUNKS], [1, F_BLOCK * HALF_B]],
                )).then_inc(gram_loaded[k % GRAM_BUFFERS], 16)

            def reload_gram(k):
                old = k - GRAM_BUFFERS
                if is_plain(old):
                    sp.wait_ge(gram_used, old + 1)
                else:
                    sp.wait_ge(gram_split, splits_before(old) + 1)
                load_gram(k)

            def load_w2(part, groups_used):
                sp.wait_ge(used, Group(end, groups_used).count(4))
                sp.dma_start(w2_parts[part], w2[:, part * W2_PART:(part + 1) * W2_PART, :]).then_inc(w2_in[part], 16)

            for i in range(4, SHIFTS - 1):
                load_shift(end, i)
            store_gram(end.plus(-2), 1)
            load_shift(end, SHIFTS - 1)
            load_w2(1, 1)
            load_w2(2, 2)
            store_gram(end.plus(-1), 0)
            load_w2(3, 3)
            sp.wait_ge(copied, CHUNKS * COPIES)
            sp.dma_start(wt2_sb, wt2).then_inc(wt2_in, 16)
            sp.wait_ge(gram_stored, 2 * 16 * (CHUNKS - 2))
            sp.wait_ge(used, QUAD * ALL_GROUPS)
            load_gram(0)
            store_gram(end.plus(-1), 1)
            load_gram(1)
            load_gram(2)
            store_gram(end, 0)
            sp.wait_ge(x0_turned, CHUNKS)
            load_gram(3)
            load_gram(4)
            reload_gram(5)
            reload_gram(6)
            store_gram(end, 1)
            reload_gram(7)
            sp.wait_ge(gram_stored, 2 * 16 * CHUNKS)
            for k in range(HALF_BLOCKS, GRAM_BLOCKS):
                reload_gram(k)
            sp.wait_ge(y_ready, 1)
            sp.dma_start(out.rearrange("b o -> o b"), y_sb).then_inc(y_stored, 16)
            sp.wait_ge(y_stored, 16)
            sp.wait_ge(x1_stored, 32 * CHUNKS)

        @block.gpsimd
        def _(pool):
            def begin_gathers(c):
                pool.wait_ge(rows_copied, c.count(1, 1))
                pool.sem_inc(gather_begun, 1)

            def gather(c, js):
                for j in js:
                    pool.indirect_dma_start(
                        out=emb[:, c.par, j * EMBED:(j + 1) * EMBED], out_offset=None, in_=tables,
                        in_offset=bass.IndirectOffsetOnAxis(ap=rows_chunk[:, c.par, j:j + 1], axis=0),
                    ).then_inc(gathered[c.par], 16)

            def low_part(g, pos):
                slot = SPLIT_SLOT[pos]
                pool.wait_ge(rounded, g.count(2, (pos + 1) // 2))
                pool.tensor_tensor(z_lo[:, slot], z[:, Z_SLOT[pos]], z_hi[:, slot].bitcast(F32),
                                   ALU.subtract).then_inc(subtracted, 1)

            def round_(c, look_up=True, groups=GROUPS):
                done = 0
                for j in range(groups):
                    for pos in (1, 3):
                        low_part(Group(c, j), pos)
                        if look_up and done == 0:
                            begin_gathers(c.plus(2))
                        if look_up:
                            upto = -(-HALF_B * (2 * j + pos // 2 + 1) // (2 * groups))
                            gather(c.plus(2), range(done, upto))
                            done = upto

            for c in (Chunk(0, 0), Chunk(0, 1)):
                begin_gathers(c)
                gather(c, range(HALF_B))
            low_part(layer1_group(Chunk(0, 0)), 3)
            with pool.Fori(0, (CHUNKS - 2) // 2) as n:
                round_(Chunk(n, 0))
                round_(Chunk(n, 1))
            round_(Chunk(0, CHUNKS - 2), look_up=False)
            round_(Chunk(0, CHUNKS - 1), look_up=False, groups=L2_GROUPS)

        @block.vector
        def _(dve):
            dve.wait_ge(ids_in, 32)
            for part, cols in enumerate((slice(0, 2 * HALF_B), slice(2 * HALF_B, CHUNKS * HALF_B))):
                step = 3 * part
                dve.tensor_scalar(ids_tmp[:, cols], ids_sb[:, cols], 0.0, info_sb[:, 0:1], ALU.is_lt, ALU.mult).then_inc(rows_step, 1)
                dve.wait_ge(rows_step, step + 1)
                dve.tensor_tensor(rows_f[:, cols], ids_tmp[:, cols], ids_sb[:, cols], ALU.add).then_inc(rows_step, 1)
                dve.wait_ge(rows_step, step + 2)
                dve.tensor_scalar(ids_tmp[:, cols], rows_f[:, cols], 0.0, info_sb[:, 1:2], ALU.max, ALU.min).then_inc(rows_step, 1)
                dve.wait_ge(rows_step, step + 3)
                dve.tensor_scalar(rows[:, cols], ids_tmp[:, cols], info_sb[:, 2:3], None, ALU.add).then_inc(rows_ready, 1)
            dve.wait_ge(w0_in, 64)
            w0_flat = w0_sb[:, :, :].rearrange("p t o -> p (t o)")
            dve.tensor_tensor(w_whole[:, 0:L1_SPLIT, :], w_whole[:, 0:L1_SPLIT, :], w0b_split_stage, ALU.add).then_inc(w0_summed, 1)
            dve.tensor_tensor(w0_flat, w0_flat, w0b_stage, ALU.add).then_inc(w0_summed, 1)

            def split_weights(step, tiles):
                dve.wait_ge(w_rounded, step)
                dve.tensor_tensor(w_lo[:, tiles, :], w_whole[:, tiles, :], w_hi[:, tiles, :].bitcast(F32),
                                  ALU.subtract).then_inc(w_split, 1)

            split_weights(1, slice(0, L1_SPLIT))
            split_weights(2, slice(L1_SPLIT, SPLIT_TILES))
            dve.wait_ge(const_in, 48)
            dve.tensor_scalar(bias3_sb[:, :], bias_sb[:, 2:3], float(EMBED), None, ALU.mult).then_inc(bias3_ready, 1)
            dve.wait_ge(w0_summed, 2)

            def times(bank, tiles, x0_tiles):
                return operand[bank][:, :].rearrange("p (q n) -> p q n", q=1).to_broadcast([P, tiles, COLS]), x0_tiles

            def form(g, pos, bank, x0_tiles):
                if not g.is_first:
                    if pos == 0:
                        dve.wait_ge(used, g.count(4, -3))
                    else:
                        dve.wait_ge(subtracted, g.count(2, -2 + (pos + 1) // 2))
                dve.tensor_tensor(z[:, Z_SLOT[pos]], *times(bank, QUAD, x0_tiles), ALU.mult).then_inc(formed, 1)

            def form_half(g, half, bank, x0_tiles):
                if not g.is_first or half:
                    dve.wait_ge(halves_split, g.count(2, half))
                dve.tensor_tensor(z_ps[:, :, :], *times(bank, 2, x0_tiles), ALU.mult).then_inc(halves_formed, 1)

            def split_half(g, half):
                dve.wait_ge(halves_rounded, g.count(2, half + 1))
                tiles = slice(2 * half, 2 * half + 2)
                dve.tensor_tensor(z_lo[:, SPLIT_SLOT[2], tiles], z_ps[:, :, :],
                                  z_hi[:, SPLIT_SLOT[2], tiles].bitcast(F32), ALU.subtract).then_inc(halves_split, 1)

            def layer1(c, pos, half=None):
                g, pair = layer1_group(c), L1_PAIR[pos]
                if half != 1:
                    dve.wait_ge(copied, g.copies(pair + 1))
                if pair == 0:
                    dve.wait_ge(x0_loaded[c.par], c.turn(16, 16))
                if half is None:
                    form(g, pos, pair % 2, x0_shift[:, c.par, 1:5])
                else:
                    form_half(g, half, pair % 2, x0_shift[:, c.par, 1 + 2 * half:3 + 2 * half])

            def layer2(c, i, pos, half=None):
                g = layer2_group(c, i)
                if pos in (1, 2) and half != 1:
                    dve.wait_ge(copied, g.copies(pos // 2 + 1))
                if i == 0 and pos == 1:
                    dve.wait_ge(x0_rest_loaded[c.par], c.turn(32, 32))
                tile = QUAD * (pos % 2)
                if half is None:
                    form(g, pos, pos // 2, x0_shift[:, c.par, tile:tile + QUAD])
                else:
                    form_half(g, half, pos // 2, x0_shift[:, c.par, tile + 2 * half:tile + 2 * half + 2])

            def form_block(c, b):
                if b == 0:
                    dve.wait_ge(x0_turned, c.count(1, 1))
                if not (c.is_(0) and b < 2):
                    dve.wait_ge(gram_done, c.count(BLOCKS, b - 1))
                dve.tensor_tensor(
                    blocks[:, b % 2], x0t_ps[:, b:b + 1, :].to_broadcast([P, GROUP_B, FIELDS]),
                    mask_sb[:, :].rearrange("p (b f) -> p b f", f=1).to_broadcast([P, GROUP_B, FIELDS]),
                    ALU.mult).then_inc(block_ready, 1)

            def sum1(c):
                dve.wait_ge(x1_ready, c.count(1, 1))
                dve.tensor_reduce(sums[:, 0, bass.ds(c.count(CHUNK_B), CHUNK_B)],
                                  x1[:, :].rearrange("p (b d) -> p b d", d=EMBED), AX.X, ALU.add).then_inc(sum1_ready, 1)

            def sum2(c):
                dve.wait_ge(x2_ready, c.count(1, 1))
                dve.tensor_reduce(sums[:, 1, bass.ds(c.count(CHUNK_B), CHUNK_B)],
                                  x2[:, :].rearrange("p (b d) -> p b d", d=EMBED), AX.X, ALU.add).then_inc(sum2_ready, 1)

            def layer2_middle(c, i):
                layer2(c, i, 2, half=0)
                layer2(c, i, 3)
                split_half(layer2_group(c, i), 0)
                layer2(c, i, 2, half=1)

            def layer1_middle(c):
                layer1(c, 2, half=0)
                layer1(c, 3)
                split_half(layer1_group(c), 0)
                layer1(c, 2, half=1)

            def round_(c):
                prev, nxt = c.plus(-1), c.plus(1)
                layer2_middle(c, 0)
                layer2(c, 1, 1)
                split_half(layer2_group(c, 0), 1)
                sum1(c)
                layer2(c, 1, 0)
                layer2_middle(c, 1)
                form_block(prev, 0)
                layer1(nxt, 1)
                split_half(layer2_group(c, 1), 1)
                sum2(prev)
                layer1(nxt, 0)
                form_block(prev, 1)
                layer1_middle(nxt)
                form_block(prev, 2)
                layer2(c, 2, 1)
                split_half(layer1_group(nxt), 1)
                layer2(c, 2, 0)
                layer2_middle(c, 2)
                layer2(c, 3, 1)
                split_half(layer2_group(c, 2), 1)
                layer2(c, 3, 0)
                layer2_middle(c, 3)
                form_block(prev, 3)
                layer2(nxt, 0, 1)
                split_half(layer2_group(c, 3), 1)
                layer2(nxt, 0, 0)

            c0, c1 = Chunk(0, 0), Chunk(0, 1)
            g0 = layer1_group(c0)
            layer1(c0, 1)
            layer1(c0, 0)
            dve.wait_ge(rounded, 1)
            dve.tensor_tensor(z_lo[:, SPLIT_SLOT[1]], z[:, Z_SLOT[1]], z_hi[:, SPLIT_SLOT[1]].bitcast(F32),
                              ALU.subtract).then_inc(subtracted, 1)
            layer1_middle(c0)
            split_half(g0, 1)
            layer1(c1, 1)
            layer1(c1, 0)
            layer1_middle(c1)
            split_half(layer1_group(c1), 1)
            sum1(c0)
            layer2(c0, 0, 1)
            layer2(c0, 0, 0)
            for i in range(L2_GROUPS):
                layer2_middle(c0, i)
                after = (c0, i + 1) if i < L2_GROUPS - 1 else (c1, 0)
                layer2(*after, 1)
                split_half(layer2_group(c0, i), 1)
                layer2(*after, 0)
            round_(c1)
            with dve.Fori(0, (CHUNKS - 4) // 2) as n:
                round_(Chunk(n, 2))
                round_(Chunk(n, 3))
            end = Chunk(0, CHUNKS - 1)
            round_(end.plus(-1))
            prev = end.plus(-1)
            layer2_middle(end, 0)
            layer2(end, 1, 1)
            split_half(layer2_group(end, 0), 1)
            sum1(end)
            layer2(end, 1, 0)
            layer2_middle(end, 1)
            form_block(prev, 0)
            layer2(end, 2, 1)
            split_half(layer2_group(end, 1), 1)
            sum2(prev)
            layer2(end, 2, 0)
            form_block(prev, 1)
            layer2_middle(end, 2)
            form_block(prev, 2)
            layer2(end, 3, 1)
            split_half(layer2_group(end, 2), 1)
            layer2(end, 3, 0)
            form_block(prev, 3)
            layer2_middle(end, 3)
            split_half(layer2_group(end, 3), 1)
            form_block(end, 0)
            form_block(end, 1)
            sum2(end)

            def split_w2(part):
                tiles = slice((part - 1) * W2_PART, part * W2_PART)
                dve.wait_ge(w2_rounded, part)
                dve.tensor_tensor(w_lo[:, tiles, :], w_whole[:, tiles, :], w_hi[:, tiles, :].bitcast(F32),
                                  ALU.subtract).then_inc(w2_split, 1)

            split_w2(1)
            form_block(end, 2)
            split_w2(2)
            form_block(end, 3)
            split_w2(3)
            for k in range(GRAM_BLOCKS):
                if not is_plain(k):
                    n = splits_before(k)
                    dve.wait_ge(gram_rounded, n + 1)
                    dve.tensor_tensor(gram_lo[n % GRAM_SLOTS], gram_buffers[k % GRAM_BUFFERS],
                                      gram_hi[n % GRAM_SLOTS].bitcast(F32), ALU.subtract).then_inc(gram_split, 1)

        @block.scalar
        def _(act):
            def to_bank(g, n, bank, released=None):
                slot = g.land_slot(n)
                act.wait_ge(landed[slot], g.landed(n))
                if released is not None:
                    act.wait_ge(*released)
                act.activation(operand[bank][:, :], land[:, slot, :], ACT.Copy).then_inc(copied, 1)

            def released_by_layer2(g, bank):
                return (formed, g.count(3, 2)) if bank == 0 else (halves_formed, g.count(2, 2))

            def released_by_layer1(g, bank):
                return (halves_formed, g.count(2, 2)) if bank == 0 else (formed, g.count(3, 3))

            def take_rows(c):
                if c.is_(0) or c.is_(2):
                    act.wait_ge(rows_ready, 1 if c.is_(0) else 2)
                if not (c.is_(0) or c.is_(1)):
                    act.wait_ge(x0_stored[c.par], c.turn(32))
                    act.sem_inc(rows_free, 1)
                act.activation(rows_chunk[:, c.par, :], rows[:, bass.ds(c.count(HALF_B), HALF_B)], ACT.Copy).then_inc(rows_copied, 1)

            def round_unit(g, pos):
                act.wait_ge(formed, g.count(3, pos))
                if not g.is_first:
                    act.wait_ge(used, g.count(4, pos - 3))
                act.activation(z_hi[:, SPLIT_SLOT[pos]], z[:, Z_SLOT[pos]], ACT.Copy).then_inc(rounded, 1)

            def round_half(g, half):
                act.wait_ge(halves_formed, g.count(2, half + 1))
                if not g.is_first:
                    if half == 0:
                        act.wait_ge(half_used, g.count(1))
                    else:
                        act.wait_ge(used, g.count(4, -1))
                act.activation(z_hi[:, SPLIT_SLOT[2], 2 * half:2 * half + 2], z_ps[:, :, :], ACT.Copy).then_inc(halves_rounded, 1)

            def square(c):
                if not c.is_(0):
                    act.wait_ge(used, layer1_group(c.plus(-1)).count(4, 1))
                act.activation(z_sq[:, :], land[0:FIELDS, layer1_group(c).land_slot(0), :], ACT.Square).then_inc(squared, 1)

            def take_x1(c):
                act.wait_ge(used, layer1_group(c).count(4, 4))
                if not c.is_(0):
                    act.wait_ge(x1_stored, c.count(32))
                    act.wait_ge(sum1_ready, c.count(1))
                act.activation(x1[:, :], acc1[:, :], ACT.Identity, bias=bias_sb[:, 0:1]).then_inc(x1_ready, 1)

            def take_x2(c):
                act.wait_ge(used, layer2_group(c, 3).count(4, 4))
                if not c.is_(0):
                    act.wait_ge(sum2_ready, c.count(1))
                    act.wait_ge(x2_turned, c.count(1))
                act.activation(x2[:, :], acc2[:, :], ACT.Identity, bias=bias_sb[:, 1:2]).then_inc(x2_ready, 1)

            def take_x2t(c):
                act.wait_ge(x2_turned, c.count(1, 1))
                if not c.is_(0):
                    act.wait_ge(gram_done, c.count(BLOCKS))
                act.activation(x2t[:, :], turn_gram_ps[:, :], ACT.Copy).then_inc(x2t_ready, 1)

            def take_gram(c, b):
                act.wait_ge(gram_done, c.count(BLOCKS, b + 1))
                if b % 2 == 0 and not (c.is_(0) and b == 0):
                    act.wait_ge(gram_stored, c.count(32, 16 * (b // 2)))
                act.activation(gram[:, :, b % 2 * GROUP_B:(b % 2 + 1) * GROUP_B].rearrange("p f b -> p b f"),
                               turn_gram_ps[:, :].rearrange("p (b f) -> p b f", f=FIELDS), ACT.Copy).then_inc(gram_staged, 1)

            def round_(c, look_up=True):
                prev, nxt = c.plus(-1), c.plus(1)
                a, b, m, d, e, f = (layer2_group(c, 0), layer2_group(c, 1), layer1_group(nxt),
                                    layer2_group(c, 2), layer2_group(c, 3), layer2_group(nxt, 0))
                to_bank(b, 0, 0, released_by_layer2(a, 0))
                if look_up:
                    take_rows(c.plus(2))
                round_half(a, 0)
                take_x2(prev)
                round_unit(a, 3)
                if not c.is_(1):
                    take_gram(c.plus(-2), 3)
                round_half(a, 1)
                to_bank(b, 1, 1, released_by_layer2(a, 1))
                round_unit(b, 1)

                to_bank(m, 0, 0, released_by_layer2(b, 0))
                round_half(b, 0)
                take_x2t(prev)
                round_unit(b, 3)
                square(nxt)
                round_half(b, 1)
                to_bank(m, 1, 1, released_by_layer2(b, 1))
                to_bank(m, 2, 0, (formed, m.count(3, 1)))
                round_unit(m, 1)

                to_bank(m, 3, 1, (formed, m.count(3, 2)))
                round_half(m, 0)
                take_gram(prev, 0)
                round_unit(m, 3)
                to_bank(d, 0, 0, released_by_layer1(m, 0))
                round_half(m, 1)
                to_bank(d, 1, 1, released_by_layer1(m, 1))
                round_unit(d, 1)

                to_bank(e, 0, 0, released_by_layer2(d, 0))
                round_half(d, 0)
                round_unit(d, 3)
                take_x1(nxt)
                take_gram(prev, 1)
                round_half(d, 1)
                to_bank(e, 1, 1, released_by_layer2(d, 1))
                round_unit(e, 1)

                round_half(e, 0)
                to_bank(f, 0, 0, released_by_layer2(e, 0))
                round_unit(e, 3)
                take_gram(prev, 2)
                round_half(e, 1)
                to_bank(f, 1, 1, released_by_layer2(e, 1))
                round_unit(f, 1)

            c0, c1 = Chunk(0, 0), Chunk(0, 1)
            g0, g1 = layer1_group(c0), layer1_group(c1)
            take_rows(c0)
            take_rows(c1)
            act.wait_ge(w0_summed, 1)
            act.activation(w_hi[:, 0:L1_SPLIT, :], w_whole[:, 0:L1_SPLIT, :], ACT.Copy).then_inc(w_rounded, 1)
            act.wait_ge(w1_split_in, 16)
            act.activation(w_hi[:, L1_SPLIT:, :], w_whole[:, L1_SPLIT:, :], ACT.Copy).then_inc(w_rounded, 1)
            to_bank(g0, 0, 0)
            to_bank(g0, 1, 1)
            square(c0)
            to_bank(g0, 2, 0, (formed, 1))
            round_unit(g0, 1)
            to_bank(g0, 3, 1, (formed, 2))
            round_half(g0, 0)
            round_unit(g0, 3)
            round_half(g0, 1)
            take_rows(c0.plus(2))
            to_bank(g1, 0, 0, released_by_layer1(g0, 0))
            to_bank(g1, 1, 1, released_by_layer1(g0, 1))
            square(c1)
            act.wait_ge(const_in, 48)
            to_bank(g1, 2, 0, (formed, g1.count(3, 1)))
            round_unit(g1, 1)
            take_x1(c0)
            to_bank(g1, 3, 1, (formed, g1.count(3, 2)))
            round_half(g1, 0)
            round_unit(g1, 3)
            round_half(g1, 1)
            first = layer2_group(c0, 0)
            to_bank(first, 0, 0, released_by_layer1(g1, 0))
            to_bank(first, 1, 1, released_by_layer1(g1, 1))
            round_unit(first, 1)
            for i in range(L2_GROUPS):
                g = layer2_group(c0, i)
                after = layer2_group(c0, i + 1) if i < L2_GROUPS - 1 else layer2_group(c1, 0)
                to_bank(after, 0, 0, released_by_layer2(g, 0))
                round_half(g, 0)
                round_unit(g, 3)
                if i == 0:
                    take_x1(c1)
                round_half(g, 1)
                to_bank(after, 1, 1, released_by_layer2(g, 1))
                round_unit(after, 1)
            round_(c1)
            with act.Fori(0, (CHUNKS - 4) // 2) as n:
                round_(Chunk(n, 2))
                round_(Chunk(n, 3))
            end = Chunk(0, CHUNKS - 1)
            prev = end.plus(-1)
            round_(prev, look_up=False)
            for i in range(L2_GROUPS):
                g = layer2_group(end, i)
                after = layer2_group(end, i + 1) if i < L2_GROUPS - 1 else None
                if after:
                    to_bank(after, 0, 0, released_by_layer2(g, 0))
                round_half(g, 0)
                if i == 0:
                    take_x2(prev)
                if i == 1:
                    take_x2t(prev)
                if i == 2:
                    take_gram(prev, 0)
                round_unit(g, 3)
                if i == 0:
                    take_gram(end.plus(-2), 3)
                if i == 3:
                    take_gram(prev, 1)
                round_half(g, 1)
                if after:
                    to_bank(after, 1, 1, released_by_layer2(g, 1))
                    round_unit(after, 1)
            take_gram(prev, 2)
            take_x2(end)
            take_gram(prev, 3)

            def round_w2(part):
                tiles = slice((part - 1) * W2_PART, part * W2_PART)
                act.wait_ge(w2_in[part], 16)
                act.activation(w_hi[:, tiles, :], w_whole[:, tiles, :], ACT.Copy).then_inc(w2_rounded, 1)

            def round_gram(k):
                if is_plain(k):
                    return
                n = splits_before(k)
                act.wait_ge(gram_loaded[k % GRAM_BUFFERS], 16 * (k // GRAM_BUFFERS + 1))
                if n >= GRAM_SLOTS:
                    act.wait_ge(gram_used, 1 + [j for j in range(k) if not is_plain(j)][n - GRAM_SLOTS])
                act.activation(gram_hi[n % GRAM_SLOTS], gram_buffers[k % GRAM_BUFFERS], ACT.Copy).then_inc(gram_rounded, 1)

            round_w2(1)
            take_x2t(end)
            take_gram(end, 0)
            round_w2(2)
            take_gram(end, 1)
            round_w2(3)
            round_gram(2)
            take_gram(end, 2)
            round_gram(3)
            take_gram(end, 3)
            for k in range(4, GRAM_BLOCKS):
                round_gram(k)
            act.wait_ge(gram_used, GRAM_BLOCKS)
            act.wait_ge(bias3_ready, 1)
            act.activation(sums[:, 2, :], z_ps[:, 1, :], ACT.Identity, bias=bias3_sb[:, 0:1]).then_inc(sum3_ready, 1)
            act.wait_ge(top_in, 6 * 16)
            for m, bank in enumerate((acc1[:, :], operand[0][:, :], operand[1][:, :], z_ps[:, 0, :])):
                act.wait_ge(top1_done, m + 1)
                act.activation(h1[:, m, :], bank, ACT.Relu, bias=bt1_sb[:, m:m + 1]).then_inc(h1_ready, 1)
            for m, bank in enumerate((turn_gram_ps[:, :], x0t_ps[:, :, :].rearrange("p b f -> p (b f)"))):
                act.wait_ge(top2_done, m + 1)
                act.activation(h2[:, m, :], bank, ACT.Relu, bias=bt2_sb[:, m:m + 1]).then_inc(h2_ready, 1)
            act.wait_ge(top3_done, 1)
            act.activation(y_sb, acc2[0:1, :], ACT.Copy).then_inc(y_ready, 1)

        @block.tensor
        def _(pe):
            def float_unit(g, acc, weights, tile0, start=False):
                pe.wait_ge(formed, g.count(3, 2))
                for q in range(QUAD):
                    mm = pe.matmul(acc[:, :], weights[:, tile0 + q, :], z[:, Z_SLOT[0], q, :], start=start and q == 0, stop=False)
                mm.then_inc(used, 1)

            def split_tile(acc, tile, slot, q, stop):
                for n, (w, zz) in enumerate(((w_hi, z_hi), (w_hi, z_lo), (w_lo, z_hi))):
                    mm = pe.matmul(acc[:, :], w[:, tile, :], zz[:, slot, q, :], start=False, stop=stop and n == 2)
                return mm

            def split_unit(g, pos, acc, tile0, stop=False):
                pe.wait_ge(subtracted, g.count(2, (pos + 1) // 2))
                for q in range(QUAD):
                    mm = split_tile(acc, tile0 + q, SPLIT_SLOT[pos], q, stop and q == QUAD - 1)
                mm.then_inc(used, 1)

            def halves_unit(g, acc, tile0):
                for half, done in enumerate((half_used, used)):
                    pe.wait_ge(halves_split, g.count(2, half + 1))
                    for q in (2 * half, 2 * half + 1):
                        mm = split_tile(acc, tile0 + q, SPLIT_SLOT[2], q, False)
                    mm.then_inc(done, 1)

            def layer1(c):
                g = layer1_group(c)
                pe.wait_ge(squared, c.count(1, 1))
                if not c.is_(0):
                    pe.wait_ge(x1_ready, c.count(1))
                pe.matmul(acc1[:, :], w0_sb[0:FIELDS, L1_PLAIN, :], z_sq[:, :], start=True, stop=False)
                float_unit(g, acc1, w0_sb, 0)
                split_unit(g, 1, acc1, 0)
                halves_unit(g, acc1, QUAD)
                split_unit(g, 3, acc1, 2 * QUAD, stop=True)

            def layer2(c, i, positions):
                g = layer2_group(c, i)
                for pos in positions:
                    tile0 = L1_SPLIT + (SPLIT_UNITS * i + pos - 1) * QUAD
                    if pos == 0:
                        if i == 0 and not c.is_(0):
                            pe.wait_ge(x2_ready, c.count(1))
                        float_unit(g, acc2, w1_sb, QUAD * i, start=i == 0)
                    elif pos == 2:
                        halves_unit(g, acc2, tile0)
                    else:
                        if i == L2_GROUPS - 1 and pos == 3 and not c.is_(0):
                            pe.wait_ge(block_ready, c.count(BLOCKS))
                        split_unit(g, pos, acc2, tile0, stop=i == L2_GROUPS - 1 and pos == 3)

            def turn_x0(c):
                for b in range(BLOCKS):
                    t = pe.transpose(x0t_ps[:, b, :], x0_shift[0:FIELDS, c.par, 0, b * P:(b + 1) * P],
                                     ident_sb[0:FIELDS, 0:FIELDS])
                t.then_inc(x0_turned, 1)

            def turn_x2(c):
                if not c.is_(0):
                    pe.wait_ge(gram_staged, c.count(BLOCKS))
                pe.wait_ge(x2_ready, c.count(1, 1))
                for b in range(BLOCKS):
                    t = pe.transpose(turn_gram_ps[:, b * P:(b + 1) * P], x2[:, b * P:(b + 1) * P], ident_sb[:, :])
                t.then_inc(x2_turned, 1)

            def gram_of(c, b):
                if b == 0:
                    pe.wait_ge(x2t_ready, c.count(1, 1))
                else:
                    pe.wait_ge(gram_staged, c.count(BLOCKS, b))
                pe.wait_ge(block_ready, c.count(BLOCKS, b + 1))
                pe.matmul(turn_gram_ps[:, :], x2t[:, b * P:(b + 1) * P],
                          blocks[:, b % 2].rearrange("p b f -> p (b f)"), start=True, stop=True).then_inc(gram_done, 1)

            def round_(c, last=False):
                prev = c.plus(-1)
                layer2(c, 0, (0, 1))
                turn_x2(prev)
                layer2(c, 0, (2, 3))
                layer2(c, 1, (0,))
                gram_of(prev, 0)
                layer2(c, 1, (1, 2, 3))
                if not last:
                    layer1(c.plus(1))
                layer2(c, 2, (0,))
                gram_of(prev, 1)
                layer2(c, 2, (1, 2, 3))
                layer2(c, 3, (0,))
                gram_of(prev, 2)
                layer2(c, 3, (1, 2, 3))
                turn_x0(c)
                gram_of(prev, 3)

            c0 = Chunk(0, 0)
            pe.wait_ge(w0_summed, 2)
            pe.wait_ge(w_split, 1)
            layer1(c0)
            layer1(c0.plus(1))
            pe.wait_ge(w1_in, 16)
            pe.wait_ge(w_split, 2)
            pe.wait_ge(const_in, 48)
            for i in range(L2_GROUPS):
                layer2(c0, i, range(QUAD))
            turn_x0(c0)
            round_(c0.plus(1))
            with pe.Fori(0, (CHUNKS - 4) // 2) as n:
                round_(Chunk(n, 2))
                round_(Chunk(n, 3))
            end = Chunk(0, CHUNKS - 1)
            round_(end.plus(-1))
            round_(end, last=True)

            top_banks = (acc1[:, :], operand[0][:, :], operand[1][:, :], z_ps[:, 0, :])

            def top1_begin(m):
                pe.matmul(top_banks[m], wt1d_sb[:, m * P:(m + 1) * P], dense_sb, start=True, stop=False)
                pe.matmul(top_banks[m], wt1_sb[:, 0, m * P:(m + 1) * P], sums[:, 0, :], start=False, stop=False)

            pe.wait_ge(top_in, 6 * 16)
            pe.wait_ge(sum1_ready, CHUNKS)
            pe.wait_ge(halves_split, 2 * ALL_GROUPS)
            half_b = BATCH // 2

            def layer3(k):
                half, fb = k // HALF_BLOCKS, k % HALF_BLOCKS
                acc = z_ps[:, 1, half * half_b:(half + 1) * half_b]
                first, last = fb == 0, fb == HALF_BLOCKS - 1
                if is_plain(k):
                    pe.wait_ge(gram_loaded[k % GRAM_BUFFERS], 16 * (k // GRAM_BUFFERS + 1))
                    pe.wait_ge(w2_in[0], 16)
                    for f in range(F_BLOCK):
                        mm = pe.matmul(acc, w2_parts[0][:, fb * F_BLOCK + f, :], gram_buffers[k % GRAM_BUFFERS][:, :, f, :],
                                       start=first and f == 0, stop=False)
                else:
                    n = splits_before(k)
                    slot = n % GRAM_SLOTS
                    pe.wait_ge(gram_split, n + 1)
                    pe.wait_ge(w2_split, fb * F_BLOCK // W2_PART)
                    for f in range(F_BLOCK):
                        tile = (fb - PLAIN_BLOCKS) * F_BLOCK + f
                        for m, (w, g) in enumerate(((w_hi, gram_hi), (w_hi, gram_lo), (w_lo, gram_hi))):
                            mm = pe.matmul(acc, w[:, tile, :], g[slot][:, :, f, :], start=False,
                                           stop=last and f == F_BLOCK - 1 and m == 2)
                mm.then_inc(gram_used, 1)

            top1_begin(0)
            turn_x2(end)
            top1_begin(1)
            gram_of(end, 0)
            top1_begin(2)
            gram_of(end, 1)
            top1_begin(3)
            layer3(0)
            gram_of(end, 2)
            layer3(1)
            gram_of(end, 3)
            pe.wait_ge(sum2_ready, CHUNKS)
            for m in range(TOP1 // P):
                pe.matmul(top_banks[m], wt1_sb[:, 1, m * P:(m + 1) * P], sums[:, 1, :], start=False, stop=False)
            for k in range(2, GRAM_BLOCKS):
                layer3(k)

            pe.wait_ge(sum3_ready, 1)
            for m in range(TOP1 // P):
                pe.matmul(top_banks[m], wt1_sb[:, 2, m * P:(m + 1) * P], sums[:, 2, :],
                          start=False, stop=True).then_inc(top1_done, 1)
            pe.wait_ge(wt2_in, 16)
            for m, bank in enumerate((turn_gram_ps[:, :], x0t_ps[:, :, :].rearrange("p b f -> p (b f)"))):
                for k in range(TOP1 // P):
                    if m == 0:
                        pe.wait_ge(h1_ready, k + 1)
                    mm = pe.matmul(bank, wt2_sb[:, k, m * P:(m + 1) * P], h1[:, k, :],
                                   start=k == 0, stop=k == TOP1 // P - 1)
                mm.then_inc(top2_done, 1)
            for k in range(TOP2 // P):
                pe.wait_ge(h2_ready, k + 1)
                mm = pe.matmul(acc2[0:1, :], wt3_sb[:, k:k + 1], h2[:, k, :], start=k == 0, stop=k == TOP2 // P - 1)
            mm.then_inc(top3_done, 1)


def shift_rows():
    p, i, k = np.meshgrid(np.arange(P), np.arange(SHIFTS), np.arange(SHIFTS), indexing="ij")
    return ((p + i) % HID) * FIELDS + (p + SHIFTS * k) % FIELDS


def pair_fields():
    p, m, k = np.meshgrid(np.arange(P), np.arange(PAIR_SHIFTS), np.arange(1, 5), indexing="ij")
    f = (p + m + PAIR_SHIFTS * (p >= FIELDS)) % FIELDS
    g = (p + SHIFTS * k) % FIELDS
    return f.reshape(P, 16), g.reshape(P, 16)


def kernel(**inputs):
    import concourse.bacc as bacc
    from concourse.bass_utils import run_bass_kernel_spmd as run

    a = {k: np.asarray(v) for k, v in inputs.items()}
    table_list = [a[f"tbl_{f}"] for f in range(FIELDS)]
    sizes = np.array([t.shape[0] for t in table_list])
    first_row = np.concatenate([[0], np.cumsum(sizes)[:-1]])
    info = np.tile(np.stack([sizes, sizes - 1, first_row], axis=1), (2, 1)).astype(np.float32)

    ids = a["ids"].reshape(CHUNKS, 2, HALF_B, FIELDS).transpose(1, 3, 0, 2).reshape(P, CHUNKS * HALF_B)

    w0 = a["L0_rec_W0"]
    f, g = pair_fields()
    once = (f - g) % FIELDS == FIELDS // 2
    pairs = w0[:, f * FIELDS + g].transpose(1, 2, 0).reshape(P, 1, QUAD, QUAD * HID)
    pairs_turned = w0[:, g * FIELDS + f].transpose(1, 2, 0)
    pairs_turned[once] = 0
    pairs_turned = pairs_turned.reshape(P, 1, QUAD, QUAD * HID)
    squares = np.zeros((P, HID), np.float32)
    squares[0:FIELDS] = w0[:, np.arange(FIELDS) * (FIELDS + 1)].T
    w1 = a["L0_rec_W1"][:, shift_rows().reshape(P, -1)].transpose(1, 2, 0).reshape(P, L2_GROUPS, QUAD, QUAD * HID)
    w2 = a["L0_rec_W2"].reshape(HID, HID, FIELDS).transpose(1, 2, 0)

    arrays = {
        "ids": ids, "field_info": info, "tables": np.concatenate(table_list, axis=0), "dense": a["dense_ctx"].T,
        "w0a": np.concatenate([pairs[:, :, 1].reshape(P, -1), squares], axis=1).reshape(P, L1_PLAIN + 1, HID),
        "w0b": np.concatenate([pairs_turned[:, :, 1].reshape(P, -1), np.zeros_like(squares)], axis=1),
        "w0a_split": pairs[:, :, [0, 2, 3]].reshape(P, L1_SPLIT, HID), "w0b_split": pairs_turned[:, :, [0, 2, 3]].reshape(P, L1_SPLIT, HID),
        "w1": w1[:, :, 0].reshape(P, L2_PLAIN, HID), "w1_split": w1[:, :, 1:].reshape(P, L2_SPLIT, HID), "w2": w2,
        "bias": np.stack([a["L0_rec_b0"], a["L0_rec_b1"], a["L0_rec_b2"]], axis=1),
        "wt1": a["W_top1"][0:3 * HID].reshape(3, P, TOP1).transpose(1, 0, 2), "wt1d": a["W_top1"][3 * HID:],
        "bt1": a["b_top1"].reshape(TOP1 // P, P).T, "wt2": a["W_top2"].reshape(TOP1 // P, P, TOP2).transpose(1, 0, 2),
        "bt2": a["b_top2"].reshape(TOP2 // P, P).T, "wt3": a["W_top3"].reshape(TOP2 // P, P).T,
        "ident": np.eye(P, dtype=np.float32),
        "mask": (np.arange(P)[:, None] // EMBED == np.arange(GROUP_B)[None, :]).astype(np.float32),
    }
    arrays = {k: np.ascontiguousarray(v) for k, v in arrays.items()}
    nc = bacc.Bacc("TRN2", target_bir_lowering=False, num_devices=1)
    aps = {k: nc.dram_tensor(f"in_{k}", v.shape, mybir.dt.from_np(v.dtype), kind="ExternalInput").ap()
           for k, v in arrays.items()}
    out = nc.dram_tensor("out_y", (BATCH, 1), F32, kind="ExternalOutput").ap()
    build(nc, out=out, **aps)
    got = run(nc, [{f"in_{k}": v for k, v in arrays.items()}], core_ids=[0])
    return got.results[0]["out_y"]
```
